# Optimizing a Trainium2 kernel written in Bass

```python
import numpy as np
import jax
import jax.numpy as jnp

def _softmax(x, axis=-1):
    return jax.nn.softmax(x, axis=axis)

def _gelu(x):
    return jax.nn.gelu(x, approximate=True)

def _silu(x):
    return jax.nn.silu(x)

def _sigmoid(x):
    return jax.nn.sigmoid(x)

def _layernorm(x, axis=-1, eps=1e-05):
    m = jnp.mean(x, axis=axis, keepdims=True)
    v = jnp.var(x, axis=axis, keepdims=True)
    return (x - m) / jnp.sqrt(v + eps)

def _scatter_add(tgt, idx, src, axis=0):
    return tgt.at[idx].add(src)

def _segment_sum(src, seg, n):
    return jax.ops.segment_sum(src, seg, n)
kernel_name = 'mk_dlrm_tower_d1_rec_r8_805dca'

def setup_inputs(seed: int=0):
    np.random.seed(seed)
    _w = jnp.asarray

    def _rec_inputs():
        import jax
        import jax.numpy as jnp
        _tk = jax.random.key(seed)
        dense_ctx = jax.random.normal(jax.random.fold_in(_tk, 190), (2048, 16), jnp.float32)
        ids = jnp.stack([jax.random.randint(jax.random.fold_in(_tk, 200 + f), (2048,), 0, v, jnp.int32) for f, v in enumerate([1000, 1000, 1250, 12500, 1000, 1250, 1250, 1000, 1000, 12500, 1000, 1000, 12500, 12500, 12500, 1000])], axis=1)
        tbl_0 = 0.05 * jax.random.normal(jax.random.fold_in(_tk, 500 + 0), (1000, 256), jnp.float32)
        tbl_1 = 0.05 * jax.random.normal(jax.random.fold_in(_tk, 500 + 1), (1000, 256), jnp.float32)
        tbl_2 = 0.05 * jax.random.normal(jax.random.fold_in(_tk, 500 + 2), (1250, 256), jnp.float32)
        tbl_3 = 0.05 * jax.random.normal(jax.random.fold_in(_tk, 500 + 3), (12500, 256), jnp.float32)
        tbl_4 = 0.05 * jax.random.normal(jax.random.fold_in(_tk, 500 + 4), (1000, 256), jnp.float32)
        tbl_5 = 0.05 * jax.random.normal(jax.random.fold_in(_tk, 500 + 5), (1250, 256), jnp.float32)
        tbl_6 = 0.05 * jax.random.normal(jax.random.fold_in(_tk, 500 + 6), (1250, 256), jnp.float32)
        tbl_7 = 0.05 * jax.random.normal(jax.random.fold_in(_tk, 500 + 7), (1000, 256), jnp.float32)
        tbl_8 = 0.05 * jax.random.normal(jax.random.fold_in(_tk, 500 + 8), (1000, 256), jnp.float32)
        tbl_9 = 0.05 * jax.random.normal(jax.random.fold_in(_tk, 500 + 9), (12500, 256), jnp.float32)
        tbl_10 = 0.05 * jax.random.normal(jax.random.fold_in(_tk, 500 + 10), (1000, 256), jnp.float32)
        tbl_11 = 0.05 * jax.random.normal(jax.random.fold_in(_tk, 500 + 11), (1000, 256), jnp.float32)
        tbl_12 = 0.05 * jax.random.normal(jax.random.fold_in(_tk, 500 + 12), (12500, 256), jnp.float32)
        tbl_13 = 0.05 * jax.random.normal(jax.random.fold_in(_tk, 500 + 13), (12500, 256), jnp.float32)
        tbl_14 = 0.05 * jax.random.normal(jax.random.fold_in(_tk, 500 + 14), (12500, 256), jnp.float32)
        tbl_15 = 0.05 * jax.random.normal(jax.random.fold_in(_tk, 500 + 15), (1000, 256), jnp.float32)
        _rk = jax.random.fold_in(_tk, 7)
        W_top1 = 0.125 * jax.random.normal(jax.random.fold_in(_tk, 801), (64, 512), jnp.float32)
        W_top2 = 0.0441942 * jax.random.normal(jax.random.fold_in(_tk, 802), (512, 256), jnp.float32)
        W_top3 = 0.0625 * jax.random.normal(jax.random.fold_in(_tk, 803), (256, 1), jnp.float32)
        b_top1 = jnp.zeros((512,), jnp.float32)
        b_top2 = jnp.zeros((256,), jnp.float32)
        return (dense_ctx, ids, tbl_0, tbl_1, tbl_2, tbl_3, tbl_4, tbl_5, tbl_6, tbl_7, tbl_8, tbl_9, tbl_10, tbl_11, tbl_12, tbl_13, tbl_14, tbl_15, W_top1, b_top1, W_top2, b_top2, W_top3)
    dense_ctx, ids, tbl_0, tbl_1, tbl_2, tbl_3, tbl_4, tbl_5, tbl_6, tbl_7, tbl_8, tbl_9, tbl_10, tbl_11, tbl_12, tbl_13, tbl_14, tbl_15, W_top1, b_top1, W_top2, b_top2, W_top3 = _rec_inputs()

    def _L0_rec_setup():
        import jax, jax.numpy as jnp
        import numpy as np
        B, F, E = (512, 16, 256)
        N_LAYERS = 3
        key = jax.random.key(seed)
        k1, k2, k3 = jax.random.split(key, 3)
        x = jax.random.normal(k1, (B, F, E), dtype=jnp.float32)
        Ws = jax.random.normal(k2, (N_LAYERS, F, F * F), dtype=jnp.float32) * 0.05
        bs = jax.random.normal(k3, (N_LAYERS, F), dtype=jnp.float32) * 0.05
        return {'x': x, 'Ws': Ws, 'bs': bs}
    _L0_rec_all = _L0_rec_setup()
    _L0_rec_in = {k: v for k, v in _L0_rec_all.items() if k in ('Ws', 'bs')}
    del _L0_rec_all
    return {'dense_ctx': dense_ctx, 'ids': ids, 'tbl_0': tbl_0, 'tbl_1': tbl_1, 'tbl_2': tbl_2, 'tbl_3': tbl_3, 'tbl_4': tbl_4, 'tbl_5': tbl_5, 'tbl_6': tbl_6, 'tbl_7': tbl_7, 'tbl_8': tbl_8, 'tbl_9': tbl_9, 'tbl_10': tbl_10, 'tbl_11': tbl_11, 'tbl_12': tbl_12, 'tbl_13': tbl_13, 'tbl_14': tbl_14, 'tbl_15': tbl_15, 'W_top1': W_top1, 'b_top1': b_top1, 'W_top2': W_top2, 'b_top2': b_top2, 'W_top3': W_top3, 'L0_rec_Ws': _L0_rec_in['Ws'], 'L0_rec_bs': _L0_rec_in['bs']}

def reference(dense_ctx, ids, tbl_0, tbl_1, tbl_2, tbl_3, tbl_4, tbl_5, tbl_6, tbl_7, tbl_8, tbl_9, tbl_10, tbl_11, tbl_12, tbl_13, tbl_14, tbl_15, W_top1, b_top1, W_top2, b_top2, W_top3, L0_rec_Ws, L0_rec_bs):
    import jax
    import jax.numpy as jnp

    def _L0_rec_ref(x, Ws, bs):
        import jax, jax.numpy as jnp
        import numpy as np
        B, F, E = (512, 16, 256)
        N_LAYERS = 3
        B_, F_, E_ = x.shape
        n_layers = Ws.shape[0]
        xk = x
        outs = []
        for i in range(n_layers):
            z = jnp.einsum('bfe,bge->bfge', x, xk).reshape(B_, F_ * F_, E_)
            z = jnp.swapaxes(z, 1, 2)
            z = jnp.einsum('bcl,oc->bol', z, Ws[i]) + bs[i][None, :, None]
            z = jax.nn.relu(z)
            z = jnp.sum(z, axis=-1)
            outs.append(z)
            xk = jnp.broadcast_to(z[:, :, None], (B_, F_, E_))
        return jnp.concatenate(outs, axis=1)
    e = jnp.stack([tbl_0[ids[:, 0]], tbl_1[ids[:, 1]], tbl_2[ids[:, 2]], tbl_3[ids[:, 3]], tbl_4[ids[:, 4]], tbl_5[ids[:, 5]], tbl_6[ids[:, 6]], tbl_7[ids[:, 7]], tbl_8[ids[:, 8]], tbl_9[ids[:, 9]], tbl_10[ids[:, 10]], tbl_11[ids[:, 11]], tbl_12[ids[:, 12]], tbl_13[ids[:, 13]], tbl_14[ids[:, 14]], tbl_15[ids[:, 15]]], axis=1)
    z = _L0_rec_ref(e, L0_rec_Ws, L0_rec_bs)
    z = z.reshape(z.shape[0], -1)
    h = jnp.concatenate([z, dense_ctx], axis=1)
    h = jnp.maximum(h @ W_top1 + b_top1, 0.0)
    h = jnp.maximum(h @ W_top2 + b_top2, 0.0)
    y = h @ W_top3
    return y

_drawn_inputs = setup_inputs


def setup_inputs(seed=0):
    import zlib

    import numpy as np

    out = dict(_drawn_inputs(seed))
    spreads = {'b_top1': (0.0, 2.0), 'b_top2': (0.0, 2.0)}
    factors = {'dense_ctx': 8.0}
    for name, (base, spread) in spreads.items():
        noise = np.random.default_rng([zlib.crc32(name.encode()), seed]).standard_normal(out[name].shape)
        drawn = base * np.exp(spread * noise) if base else spread * noise
        out[name] = jnp.asarray(drawn.astype(out[name].dtype))
    for name, factor in factors.items():
        out[name] = (out[name] * factor).astype(out[name].dtype)
    return out
```

```python
import concourse.bass as bass
from concourse import mybir
from contextlib import ExitStack

B, F, E, L, O = 2048, 16, 256, 3, 16
DENSE, H1, H2 = 16, 512, 256
P = 128
NB = B // P
NC = E // P
COLS = F * P
BANK = 512
FPB = BANK // P
NJ = COLS // BANK
TILE = P // NJ
FF = F * F
ROUNDS = [("act", 0), ("dve", 1), ("dve", 2), ("dve", 3), ("dve", 4), ("pool", 7), ("dve", 5), ("dve", 6),
          ("pool", 8)]
NR = len(ROUNDS)
DVE_ROUNDS = [r for r, (who, _) in enumerate(ROUNDS) if who == "dve"]
POOL_ROUNDS = [r for r, (who, _) in enumerate(ROUNDS) if who == "pool"]
DVE_RING = 3
BANKS = 3
NG = COLS * NC // BANK
FIRST_LOOP, LOOP_END, PERIODS = 2, (NB - 1) // 2, (NB + 3 + 1) // 2
HPAD = 128


def tower(nc, tables, ids, dense, w0, wu, bias0, bias12, identity, pick, w_top1, w_top2, w_top3, b_top1,
          b_top2, out):
    f32, i32, u32 = mybir.dt.float32, mybir.dt.int32, mybir.dt.uint32
    ALU = mybir.AluOpType
    ACT = mybir.ActivationFunctionType
    AX = mybir.AxisListType
    ds = bass.ds

    ctx = ExitStack()
    with ctx:
        def sb(name, shape, dt=f32):
            return ctx.enter_context(nc.sbuf_tensor(name, shape, dt))

        def sem(name):
            return ctx.enter_context(nc.semaphore(name))

        gathered = sb("gathered", [P, 2, F, E])
        xt = sb("xt", [P, 2, NC, COLS])
        squares = sb("squares", [P, NC, COLS])
        dve_prods = sb("dve_prods", [P, DVE_RING, NC, COLS])
        pool_prods = sb("pool_prods", [P, NC, COLS + COLS // 2])
        relus = sb("relus", [P, BANKS, BANK])
        u_sb = sb("u_sb", [P, BANK])
        ut_sb = sb("ut_sb", [P, 2, BANK])
        outer = sb("outer", [P, 2, O * FF])
        zsum = sb("zsum", [TILE, P])
        z0 = sb("z0", [P, 2, O])
        z1 = sb("z1", [P, 2, O])
        z2 = sb("z2", [P, 2, O])
        h_all = sb("h_all", [P, NB, HPAD])
        idx_all = sb("idx_all", [P, NB * F], i32)
        idx = sb("idx", [P, 2, F], i32)
        w0_sb = sb("w0_sb", [P, NC, TILE])
        wu_sb = sb("wu_sb", [P, NC, TILE])
        bias0_sb = sb("bias0_sb", [P, 1])
        bias0x2 = sb("bias0x2", [P, 1])
        bias12_sb = sb("bias12_sb", [P, 2 * O])
        ident = sb("ident", [P, P])
        pick_sb = sb("pick_sb", [P, TILE])
        wt1 = gathered[:, 0, 0:2, :].rearrange("p a b -> p (a b)")
        wt2 = gathered[:, 0, 2:6, :].rearrange("p k n -> p (k n)")
        wt3 = gathered[:, 0, 6, 0:2]
        bt1 = gathered[:, 0, 6, 2:6]
        bt2 = gathered[:, 0, 6, 6:8]
        h_in = xt[:, 0, 0, :]
        h1 = [dve_prods[:, i, 0, :].rearrange("p (m n) -> p m n", m=4) for i in range(2)]
        h2 = [dve_prods[:, i, 1, 0:1024].rearrange("p (m n) -> p m n", m=2) for i in range(2)]
        y = squares[0:1, 0, :]

        ps = [ctx.enter_context(nc.psum_tensor(f"ps{i}", [P, BANK], f32)) for i in range(8)]
        ps_round, ps_tr, ps_sum, ps_u, ps_z = ps[0:BANKS], ps[3:5], ps[5], ps[6], ps[7]

        idx_loaded = sem("idx_loaded")
        idx_ready = sem("idx_ready")
        idx_copied = sem("idx_copied")
        rows_loaded = [sem("rows_loaded0"), sem("rows_loaded1")]
        consts_loaded = sem("consts_loaded")
        bias_ready = sem("bias_ready")
        tr_done = sem("tr_done")
        xt_ready = sem("xt_ready")
        squares_ready = sem("squares_ready")
        dve_prods_ready = sem("dve_prods_ready")
        pool_prods_ready = sem("pool_prods_ready")
        round_done = sem("round_done")
        relu_ready = sem("relu_ready")
        sum_done = sem("sum_done")
        zsum_ready = sem("zsum_ready")
        zt_done = sem("zt_done")
        z0_ready = sem("z0_ready")
        u_done = sem("u_done")
        u_copied = sem("u_copied")
        ut_done = sem("ut_done")
        ut_ready = sem("ut_ready")
        outer_ready = [sem("outer1_ready"), sem("outer2_ready")]
        layer_done = [sem("layer1_done"), sem("layer2_done")]
        kept = sem("kept")
        h_zeroed = sem("h_zeroed")
        dense_loaded = sem("dense_loaded")
        top_zeroed = sem("top_zeroed")
        top_loaded = sem("top_loaded")
        ht_done = sem("ht_done")
        ht_ready = sem("ht_ready")
        mm1_done = sem("mm1_done")
        h1_ready = sem("h1_ready")
        mm2_done = sem("mm2_done")
        h2_ready = sem("h2_ready")
        mm3_done = sem("mm3_done")
        y_ready = sem("y_ready")
        stored = sem("stored")

        block = ctx.enter_context(nc.Block())
        NCONST, NTOP = 7, 5

        def periods(eng, step):
            for k in range(FIRST_LOOP):
                for s in range(2):
                    step(k, s)
            with eng.Fori(FIRST_LOOP, LOOP_END) as k:
                for s in range(2):
                    step(k, s)
            for k in range(LOOP_END, PERIODS):
                for s in range(2):
                    step(k, s)

        def has(k, s, lag):
            return not isinstance(k, int) or 0 <= 2 * k + s - lag < NB

        def wait(eng, semaphore, value):
            if not isinstance(value, int) or value > 0:
                eng.wait_ge(semaphore, value)

        def halves(d):
            if d == F // 2:
                return [(0, d * P, 0, d * P)]
            return [(0, d * P, 0, (F - d) * P), ((F - d) * P, 0, (F - d) * P, d * P)]

        @block.gpsimd
        def _(pool):
            pool.wait_ge(idx_loaded, 16)

            def gather(k, r):
                b = 2 * k + r
                if not (isinstance(k, int) and k == 0):
                    used = NG * (b - 1)
                    pool.wait_ge(tr_done, used)
                nc.gpsimd.tensor_copy(idx[:, r, :], idx_all[:, ds(F * b, F)]).then_inc(idx_copied, 1)
                copied = b + 1
                if not isinstance(k, int):
                    copied = pool.to_reg(copied)
                pool.wait_ge(idx_loaded, 16)
                pool.wait_ge(idx_copied, copied)
                for f in range(F):
                    pool.indirect_dma_start(
                        out=gathered[:, r, f, :], out_offset=None, in_=tables[f],
                        in_offset=bass.IndirectOffsetOnAxis(ap=idx[:, r, f:f + 1].bitcast(u32), axis=0),
                    ).then_inc(rows_loaded[r], 16)

            def products(k, s):
                t = 2 * k + s
                pool.wait_ge(xt_ready, NG * (t + 1))
                for i, r in enumerate(POOL_ROUNDS):
                    wait(pool, round_done, NR * (t - 1) + r + 1)
                    for c in range(NC):
                        for a, b, o, n in halves(ROUNDS[r][1]):
                            last = nc.gpsimd.tensor_tensor(pool_prods[:, c, COLS * i + o:COLS * i + o + n],
                                                           xt[:, s, c, a:a + n], xt[:, s, c, b:b + n], ALU.mult)
                    last.then_inc(pool_prods_ready, 1)

            def step(k, s):
                if has(k, s, 0):
                    products(k, s)
                if has(k, s, -2):
                    gather(k + 1, s)

            gather(0, 0)
            gather(0, 1)
            periods(pool, step)

        @block.sync
        def _(sp):
            sp.dma_start(idx_all[:], ids).then_inc(idx_loaded, 16)
            for dst, src in ((ident[:], identity), (w0_sb[:], w0), (wu_sb[:], wu), (bias0_sb[:], bias0),
                             (bias12_sb[:], bias12), (pick_sb[:], pick)):
                sp.dma_start(dst, src).then_inc(consts_loaded, 16)
            sp.wait_ge(h_zeroed, 1)
            sp.dma_start(h_all[:, :, L * O:L * O + DENSE], dense).then_inc(consts_loaded, 16)
            sp.wait_ge(top_zeroed, 1)
            for dst, src in ((wt1[0:L * O + DENSE, :], w_top1), (wt2, w_top2), (wt3, w_top3),
                             (bt1, b_top1), (bt2, b_top2)):
                sp.dma_start(dst, src).then_inc(top_loaded, 16)
            sp.wait_ge(y_ready, NJ)
            sp.dma_start(out, y).then_inc(stored, 16)
            sp.wait_ge(stored, 16)

        @block.vector
        def _(dve):
            nc.vector.memset(h_all[:], 0.0).then_inc(h_zeroed, 1)
            dve.wait_ge(consts_loaded, 16 * NCONST)
            nc.vector.tensor_tensor(bias0x2[:], bias0_sb[:], bias0_sb[:], ALU.add).then_inc(bias_ready, 1)

            def products(k, s, i):
                t, n_dve = 2 * k + s, len(DVE_ROUNDS)
                if i == 0:
                    dve.wait_ge(xt_ready, NG * (t + 1))
                if i >= DVE_RING:
                    dve.wait_ge(round_done, NR * t + DVE_ROUNDS[i - DVE_RING] + 1)
                else:
                    wait(dve, round_done, NR * (t - 1) + DVE_ROUNDS[i - DVE_RING] + 1)
                for c in range(NC):
                    for a, b, o, n in halves(ROUNDS[DVE_ROUNDS[i]][1]):
                        last = nc.vector.tensor_tensor(dve_prods[:, i % DVE_RING, c, o:o + n],
                                                       xt[:, s, c, a:a + n], xt[:, s, c, b:b + n], ALU.mult)
                last.then_inc(dve_prods_ready, 1)

            def outer_product(k, s, l):
                t = 2 * k + s
                r = (s - 1 - l) % 2
                z = (z0, z1)[l]
                dve.wait_ge((z0_ready, layer_done[0])[l], t - l)
                dve.wait_ge(ut_ready, t - l)
                wait(dve, layer_done[l], t - 1 - l)
                u = ut_sb[:, r, :].rearrange("p (f m) -> p m f", m=TILE)[:, O * l:O * (l + 1), :]
                nc.vector.tensor_tensor(
                    outer[:, l, :].rearrange("p (o f g) -> p o f g", o=O, f=F),
                    u.unsqueeze(3).to_broadcast([P, O, F, F]),
                    z[:, r, :].unsqueeze(1).unsqueeze(1).to_broadcast([P, O, F, F]),
                    ALU.mult).then_inc(outer_ready[l], 1)

            def keep(k, s, l):
                t = 2 * k + s
                if l == 2:
                    dve.wait_ge(layer_done[1], t - 2)
                nc.vector.tensor_copy(h_all[:, ds(t - 1 - l, 1), O * l:O * (l + 1)],
                                      (z0, z1, z2)[l][:, (s - 1 - l) % 2, :].unsqueeze(1)).then_inc(kept, 1)

            def step(k, s):
                t = 2 * k + s
                if has(k, s, 0):
                    products(k, s, 0)
                if has(k, s, 1):
                    dve.wait_ge(sum_done, NR * t)
                    nc.vector.tensor_reduce(out=zsum[:], in_=ps_sum[0:TILE, :].rearrange("p (f b) -> p b f", b=P),
                                            op=ALU.add, axis=AX.X).then_inc(zsum_ready, 1)
                if has(k, s, 2):
                    outer_product(k, s, 1)
                    keep(k, s, 1)
                if has(k, s, 3):
                    keep(k, s, 2)
                if has(k, s, 0):
                    products(k, s, 1)
                if has(k, s, 1):
                    dve.wait_ge(zt_done, t)
                    nc.vector.tensor_copy(z0[:, (s - 1) % 2, :], ps_z[:, 0:O]).then_inc(z0_ready, 1)
                    outer_product(k, s, 0)
                    keep(k, s, 0)
                for i in range(2, len(DVE_ROUNDS)):
                    if has(k, s, 0):
                        products(k, s, i)

            periods(dve, step)
            dve.wait_ge(round_done, NR * NB)
            nc.vector.memset(wt1, 0.0).then_inc(top_zeroed, 1)
            for n in range(NJ):
                dve.wait_ge(ht_done, n + 1)
                nc.vector.tensor_copy(h_in[:, BANK * n:BANK * (n + 1)], ps[n][:, :]).then_inc(ht_ready, 1)
            for n in range(NJ):
                dve.wait_ge(mm3_done, n + 1)
                nc.vector.tensor_copy(y[:, BANK * n:BANK * (n + 1)], ps[n % 2][0:1, :]).then_inc(y_ready, 1)

        @block.scalar
        def _(act):
            act.wait_ge(bias_ready, 1)

            def evacuate(k, r, g):
                b = 2 * k + r
                if g == 0:
                    wait(act, round_done, NR * (b - 1))
                act.wait_ge(tr_done, NG * b + g + 1)
                nc.scalar.activation(xt[:, r, g % NC, BANK * (g // NC):BANK * (g // NC + 1)], ps_tr[g % 2][:, :],
                                     ACT.Copy).then_inc(xt_ready, 1)

            def square(k, r):
                b = 2 * k + r
                act.wait_ge(xt_ready, NG * (b + 1))
                wait(act, round_done, NR * (b - 1) + 1)
                nc.scalar.activation(squares[:], xt[:, r, :, :], ACT.Square).then_inc(squares_ready, 1)

            def relu(k, s, r):
                t = 2 * k + s
                act.wait_ge(round_done, NR * t + r + 1)
                wait(act, sum_done, NR * t + r - BANKS + 1)
                n = BANK // 2 if ROUNDS[r][1] == F // 2 else BANK
                twice = ROUNDS[r][1] > 0
                nc.scalar.activation(relus[:, r % BANKS, 0:n], ps_round[r % BANKS][:, 0:n], ACT.Relu,
                                     bias=(bias0x2 if twice else bias0_sb)[:, 0:1],
                                     scale=2.0 if twice else 1.0).then_inc(relu_ready, 1)

            def layer(k, s, l, o):
                t = 2 * k + s
                if o == 0:
                    act.wait_ge(outer_ready[l], t - l)
                pre = outer[:, l, FF * o:FF * (o + 1)]
                done = nc.scalar.activation(pre, pre, ACT.Relu, bias=bias12_sb[:, O * l + o:O * l + o + 1],
                                            accum_out=(z1, z2)[l][:, (s - 1 - l) % 2, o:o + 1])
                if o == O - 1:
                    done.then_inc(layer_done[l], 1)

            def step(k, s):
                t = 2 * k + s
                for r in range(NR):
                    if r < NG and has(k, s, -1):
                        evacuate(k + (s + 1) // 2, (s + 1) % 2, r)
                    if has(k, s, 0):
                        relu(k, s, r)
                    if r == 3 and has(k, s, 0):
                        act.wait_ge(u_done, t + 1)
                        nc.scalar.activation(u_sb[:], ps_u[:, :], ACT.Copy).then_inc(u_copied, 1)
                    if r == 5 and has(k, s, 0):
                        act.wait_ge(ut_done, t + 1)
                        wait(act, outer_ready[1], t - 1)
                        nc.scalar.activation(ut_sb[:, s, :], ps_u[:, :], ACT.Copy).then_inc(ut_ready, 1)
                    if has(k, s, 2):
                        for o in range(O * r // NR, O * (r + 1) // NR):
                            layer(k, s, 1, o)
                    if r >= 2 and has(k, s, 1):
                        for o in range(O * (r - 2) // (NR - 2), O * (r - 1) // (NR - 2)):
                            layer(k, s, 0, o)
                if has(k, s, -1):
                    square(k + (s + 1) // 2, (s + 1) % 2)

            for g in range(NG):
                evacuate(0, 0, g)
            square(0, 0)
            periods(act, step)
            act.wait_ge(top_loaded, 16 * NTOP)
            for n in range(NJ):
                for m in range(4):
                    act.wait_ge(mm1_done, 4 * n + m + 1)
                    if n >= 2 and m == 0:
                        act.wait_ge(mm2_done, 2 * (n - 1))
                    nc.scalar.activation(h1[n % 2][:, m, :], ps[4 + m % 2][:, :], ACT.Relu,
                                         bias=bt1[:, m:m + 1]).then_inc(h1_ready, 1)
                for m in range(2):
                    act.wait_ge(mm2_done, 2 * n + m + 1)
                    if n >= 2 and m == 0:
                        act.wait_ge(mm3_done, n - 1)
                    nc.scalar.activation(h2[n % 2][:, m, :], ps[6 + m][:, :], ACT.Relu,
                                         bias=bt2[:, m:m + 1]).then_inc(h2_ready, 1)

        @block.tensor
        def _(pe):
            pe.wait_ge(bias_ready, 1)

            def transposes(k, r, g):
                b = 2 * k + r
                if g == 0:
                    pe.wait_ge(rows_loaded[r], 16 * F * k + 16 * F)
                wait(pe, xt_ready, NG * b + g - 1)
                for i in range(FPB):
                    last = nc.tensor.transpose(ps_tr[g % 2][:, P * i:P * (i + 1)],
                                               gathered[:, r, FPB * (g // NC) + i, P * (g % NC):P * (g % NC + 1)],
                                               ident[:])
                last.then_inc(tr_done, 1)

            def contract(k, s, r):
                t = 2 * k + s
                who, d = ROUNDS[r]
                n = BANK // 2 if d == F // 2 else BANK
                if who == "act":
                    pe.wait_ge(squares_ready, t + 1)
                    src = squares[:]
                elif who == "dve":
                    i = DVE_ROUNDS.index(r)
                    pe.wait_ge(dve_prods_ready, len(DVE_ROUNDS) * t + i + 1)
                    src = dve_prods[:, i % DVE_RING, :, :]
                else:
                    i = POOL_ROUNDS.index(r)
                    pe.wait_ge(pool_prods_ready, len(POOL_ROUNDS) * t + i + 1)
                    src = pool_prods[:, :, COLS * i:COLS * i + NJ * n]
                wait(pe, relu_ready, NR * t + r - BANKS + 1)
                for c in range(NC):
                    for j in range(NJ):
                        last = nc.tensor.matmul(ps_round[r % BANKS][TILE * j:TILE * (j + 1), 0:n],
                                                w0_sb[:, c, :], src[:, c, n * j:n * (j + 1)],
                                                start=(c == 0), stop=(c == NC - 1))
                last.then_inc(round_done, 1)

            def add_up(k, s, r):
                b = 2 * k + s
                n = BANK // 2 if ROUNDS[r][1] == F // 2 else BANK
                pe.wait_ge(relu_ready, NR * b + r + 1)
                if r == 0:
                    wait(pe, zsum_ready, b)
                nc.tensor.matmul(ps_sum[0:TILE, 0:n], pick_sb[:], relus[:, r % BANKS, 0:n],
                                 start=(r == 0), stop=(r == NR - 1)).then_inc(sum_done, 1)

            def step(k, s):
                t = 2 * k + s
                for r in range(NR):
                    if has(k, s, 0):
                        contract(k, s, r)
                    if r == 0 and has(k, s, 1):
                        add_up(k + (s - 1) // 2, (s - 1) % 2, NR - 1)
                    if r >= 1 and has(k, s, 0):
                        add_up(k, s, r - 1)
                    if r < NG and has(k, s, -1):
                        transposes(k + (s + 1) // 2, (s + 1) % 2, r)
                    if r == 2 and has(k, s, 1):
                        pe.wait_ge(zsum_ready, t)
                        nc.tensor.matmul(ps_z[:, 0:O], zsum[:], ident[0:TILE, 0:O],
                                         start=True, stop=True).then_inc(zt_done, 1)
                    if r == 2 and has(k, s, 0):
                        wait(pe, ut_ready, t)
                        pe.wait_ge(xt_ready, NG * (t + 1))
                        for c in range(NC):
                            for j in range(NJ):
                                last = nc.tensor.matmul(ps_u[TILE * j:TILE * (j + 1), :], wu_sb[:, c, :],
                                                        xt[:, s, c, BANK * j:BANK * (j + 1)],
                                                        start=(c == 0), stop=(c == NC - 1))
                        last.then_inc(u_done, 1)
                    if r == 4 and has(k, s, 0):
                        pe.wait_ge(u_copied, t + 1)
                        for i in range(FPB):
                            last = nc.tensor.transpose(ps_u[:, P * i:P * (i + 1)], u_sb[:, P * i:P * (i + 1)],
                                                       ident[:])
                        last.then_inc(ut_done, 1)

            for g in range(NG):
                transposes(0, 0, g)
            periods(pe, step)
            pe.wait_ge(kept, L * NB)
            pe.wait_ge(relu_ready, NR * NB)
            pe.wait_ge(xt_ready, NG * NB)
            for n in range(NJ):
                for i in range(FPB):
                    last = nc.tensor.transpose(ps[n][:, P * i:P * (i + 1)], h_all[:, FPB * n + i, :], ident[:])
                last.then_inc(ht_done, 1)
            pe.wait_ge(top_loaded, 16 * NTOP)
            for n in range(NJ):
                pe.wait_ge(ht_ready, n + 1)
                for m in range(4):
                    if 4 * n + m >= 2:
                        pe.wait_ge(h1_ready, 4 * n + m - 1)
                    nc.tensor.matmul(ps[4 + m % 2][:, :], wt1[:, P * m:P * (m + 1)],
                                     h_in[:, BANK * n:BANK * (n + 1)],
                                     start=True, stop=True).then_inc(mm1_done, 1)
                pe.wait_ge(h1_ready, 4 * n + 4)
                for m in range(2):
                    if n:
                        pe.wait_ge(h2_ready, 2 * n)
                    for c in range(4):
                        last = nc.tensor.matmul(ps[6 + m][:, :], wt2[:, H2 * c + P * m:H2 * c + P * (m + 1)],
                                                h1[n % 2][:, c, :], start=(c == 0), stop=(c == 3))
                    last.then_inc(mm2_done, 1)
                pe.wait_ge(h2_ready, 2 * n + 2)
                if n == 0:
                    pe.wait_ge(ht_ready, 2)
                else:
                    wait(pe, y_ready, n - 1)
                for m in range(2):
                    last = nc.tensor.matmul(ps[n % 2][0:1, :], wt3[:, m:m + 1], h2[n % 2][:, m, :],
                                            start=(m == 0), stop=(m == 1))
                last.then_inc(mm3_done, 1)


def kernel(**inputs):
    import numpy as np
    import concourse.bacc as bacc
    from concourse import mybir as mb
    from concourse.bass_utils import run_bass_kernel_spmd

    f4 = np.float32
    get = lambda n: np.asarray(inputs[n])
    Ws, bs = get("L0_rec_Ws"), get("L0_rec_bs")
    wt = Ws.reshape(L, O, NC, P).transpose(3, 2, 0, 1)
    w0 = np.zeros((P, NC, TILE), f4)
    w0[:, :, :O] = wt[:, :, 0]
    bias0 = np.zeros((NJ, TILE), f4)
    bias0[:, :O] = bs[0]
    pick = np.zeros((NJ, TILE, TILE), f4)
    pick[:, np.arange(O), np.arange(O)] = 1
    arrays = {f"tbl_{f}": get(f"tbl_{f}") for f in range(F)} | {
        "ids": np.ascontiguousarray(get("ids").reshape(NB, P, F).transpose(1, 0, 2)).reshape(P, NB * F),
        "dense": np.ascontiguousarray(get("dense_ctx").reshape(NB, P, DENSE).transpose(1, 0, 2)),
        "w0": w0,
        "wu": np.ascontiguousarray(wt[:, :, 1:].reshape(P, NC, TILE)),
        "bias0": bias0.reshape(P, 1),
        "bias12": np.ascontiguousarray(np.broadcast_to(bs[1:].reshape(1, 2 * O), (P, 2 * O))),
        "identity": np.eye(P, dtype=f4),
        "pick": pick.reshape(P, TILE),
        "w_top1": get("W_top1"),
        "w_top2": np.ascontiguousarray(get("W_top2").reshape(4, P, H2).transpose(1, 0, 2)).reshape(P, 4 * H2),
        "w_top3": np.ascontiguousarray(get("W_top3").reshape(2, P).T),
        "b_top1": np.ascontiguousarray(get("b_top1").reshape(4, P).T),
        "b_top2": np.ascontiguousarray(get("b_top2").reshape(2, P).T),
    }
    nc = bacc.Bacc("TRN2", target_bir_lowering=False, num_devices=1)
    aps = [nc.dram_tensor(f"in_{n}", a.shape, mb.dt.from_np(a.dtype), kind="ExternalInput").ap()
           for n, a in arrays.items()]
    out = nc.dram_tensor("out_y", (1, B), mb.dt.float32, kind="ExternalOutput").ap()
    tower(nc, aps[:F], *aps[F:], out)
    r = run_bass_kernel_spmd(nc, [{f"in_{n}": a for n, a in arrays.items()}], core_ids=[0])
    return np.asarray(r.results[0]["out_y"]).reshape(B, 1)
```

```python
import concourse.bass as bass
from concourse import mybir
from contextlib import ExitStack

B, F, E, L, O = 2048, 16, 256, 3, 16
DENSE, H1, H2 = 16, 512, 256
P = 128
NB = B // P
NC = E // P
COLS = F * P
BANK = 512
FPB = BANK // P
NJ = COLS // BANK
TILE = P // NJ
FF = F * F
ROUNDS = [("dve", 1), ("act", 0), ("dve", 2), ("dve", 3), ("pool", 7), ("dve", 4), ("pool", 8), ("dve", 5),
          ("dve", 6)]
NR = len(ROUNDS)
DVE_ROUNDS = [r for r, (who, _) in enumerate(ROUNDS) if who == "dve"]
POOL_ROUNDS = [r for r, (who, _) in enumerate(ROUNDS) if who == "pool"]
SHARED = len(DVE_ROUNDS) - 1
DVE_RING = 3
BANKS = 3
NG = COLS * NC // BANK
EVACUATIONS = (0, 0, 2, 2, 2, 2, 0, 0, 0)
SQUARES = (0, 0, 0, 0, 0, 0, 1, 1, 2)
LAYER2 = (0, 0, 4, 6, 4, 2, 0, 0, 0)
LAYER1 = (3, 0, 0, 0, 0, 0, 4, 4, 5)
NQ = sum(SQUARES)
CHUNKS = (4, 4, 4, 3, 1)
NJOBS = 8
TOP_SLOTS = {(NB - 1, r): [(0, r)] for r in range(NJOBS)}
TOP_SLOTS |= {(NB, r): [(1, r - 1)] for r in range(1, NR)}
TOP_SLOTS |= {(NB + 1, r): [(2, r)] for r in range(NJOBS)}
TOP_SLOTS |= {(NB + 1, NR - 1): [(n, j) for n in (3, 4) for j in range(NJOBS)]}
FIRST_LOOP, LOOP_END, PERIODS = 2, (NB - 1) // 2, (NB + 2) // 2
HPAD = 128


def tower(nc, tables, ids, dense, w0, wu, bias0, bias12, identity, pick, w_top1, w_top2, w_top3, b_top1,
          b_top2, out):
    f32, i32, u32 = mybir.dt.float32, mybir.dt.int32, mybir.dt.uint32
    ALU = mybir.AluOpType
    ACT = mybir.ActivationFunctionType
    AX = mybir.AxisListType
    ds = bass.ds

    ctx = ExitStack()
    with ctx:
        def sb(name, shape, dt=f32):
            return ctx.enter_context(nc.sbuf_tensor(name, shape, dt))

        def sem(name):
            return ctx.enter_context(nc.semaphore(name))

        gathered = sb("gathered", [P, 2, F, E])
        xt = sb("xt", [P, 2, NC, COLS])
        squares = sb("squares", [P, NC, COLS])
        dve_prods = sb("dve_prods", [P, DVE_RING, NC, COLS])
        pool_prods = sb("pool_prods", [P, NC, COLS + COLS // 2])
        relus = sb("relus", [P, BANKS, BANK])
        u_sb = sb("u_sb", [P, BANK])
        ut_sb = sb("ut_sb", [P, 2, BANK])
        outer = sb("outer", [P, 2, O * FF])
        zsum = sb("zsum", [P, P])
        z0 = sb("z0", [P, 2, O])
        z1 = sb("z1", [P, 2, O])
        z2 = sb("z2", [P, 2, O])
        h_all = sb("h_all", [P, NB, HPAD])
        idx_all = sb("idx_all", [P, NB * F], i32)
        idx = sb("idx", [P, 2, F], i32)
        w0_sb = sb("w0_sb", [P, NC, TILE])
        wu_sb = sb("wu_sb", [P, NC, TILE])
        bias0_sb = sb("bias0_sb", [P, 1])
        bias0x2 = sb("bias0x2", [P, 1])
        bias12_sb = sb("bias12_sb", [P, 2 * O])
        ident = sb("ident", [P, P])
        pick_sb = sb("pick_sb", [P, TILE])
        wt1 = gathered[:, 0, 0:2, :].rearrange("p a b -> p (a b)")
        wt2 = gathered[:, 0, 2:6, :].rearrange("p k n -> p (k n)")
        wt3 = gathered[:, 0, 6, 0:2]
        bt1 = gathered[:, 0, 6, 2:6]
        bt2 = gathered[:, 0, 6, 6:8]
        y = gathered[0:1, 0, 8:16, :].rearrange("p a b -> p (a b)")
        h_in = gathered[:, 1, 0:2, :].rearrange("p a b -> p (a b)")
        h1 = gathered[:, 1, 2:10, :].rearrange("p (m a) b -> p m (a b)", m=4)
        h2 = gathered[:, 1, 10:14, :].rearrange("p (m a) b -> p m (a b)", m=2)

        ps = [ctx.enter_context(nc.psum_tensor(f"ps{i}", [P, BANK], f32)) for i in range(8)]
        ps_round, ps_tr, ps_sum, ps_u = ps[0:BANKS], ps[3:5], ps[5:7], ps[7]

        idx_loaded = sem("idx_loaded")
        idx_ready = sem("idx_ready")
        idx_copied = sem("idx_copied")
        rows_loaded = [sem("rows_loaded0"), sem("rows_loaded1")]
        first_rows_loaded = [sem(f"first_rows_loaded{i}") for i in range(NJ)]
        consts_loaded = sem("consts_loaded")
        bias_ready = sem("bias_ready")
        tr_done = sem("tr_done")
        xt_ready = sem("xt_ready")
        squares_ready = sem("squares_ready")
        dve_prods_ready = sem("dve_prods_ready")
        pool_prods_ready = sem("pool_prods_ready")
        round_done = sem("round_done")
        relu_ready = sem("relu_ready")
        sum_done = sem("sum_done")
        zsum_ready = sem("zsum_ready")
        zt_done = sem("zt_done")
        z0_ready = sem("z0_ready")
        u_done = sem("u_done")
        u_copied = sem("u_copied")
        ut_done = sem("ut_done")
        ut_ready = sem("ut_ready")
        outer_ready = [sem("outer1_ready"), sem("outer2_ready")]
        layer_done = [sem("layer1_done"), sem("layer2_done")]
        kept = sem("kept")
        h_zeroed = sem("h_zeroed")
        dense_loaded = sem("dense_loaded")
        top_zeroed = sem("top_zeroed")
        top_loaded = sem("top_loaded")
        top_done = sem("top_done")
        top_ready = sem("top_ready")
        stored = sem("stored")

        block = ctx.enter_context(nc.Block())
        NCONST, NTOP = 7, 5

        def periods(eng, step):
            for k in range(FIRST_LOOP):
                for s in range(2):
                    step(k, s)
            with eng.Fori(FIRST_LOOP, LOOP_END) as k:
                for s in range(2):
                    step(k, s)
            for k in range(LOOP_END, PERIODS):
                for s in range(2):
                    step(k, s)

        def has(k, s, lag):
            return not isinstance(k, int) or 0 <= 2 * k + s - lag < NB

        def wait(eng, semaphore, value):
            if not isinstance(value, int) or value > 0:
                eng.wait_ge(semaphore, value)

        def slot(table, r):
            return range(sum(table[:r]), sum(table[:r + 1]))

        def layer1_slot(r):
            start = sum(LAYER1[1:r]) if r else sum(LAYER1[1:])
            return range(start, start + LAYER1[r])

        def halves(d):
            if d == F // 2:
                return [(0, d * P, 0, d * P)]
            return [(0, d * P, 0, (F - d) * P), ((F - d) * P, 0, (F - d) * P, d * P)]

        @block.gpsimd
        def _(pool):
            pool.wait_ge(idx_loaded, 16)

            def gather(k, r):
                b = 2 * k + r
                if not (isinstance(k, int) and k == 0):
                    used = NG * (b - 1)
                    pool.wait_ge(tr_done, used)
                nc.gpsimd.tensor_copy(idx[:, r, :], idx_all[:, ds(F * b, F)]).then_inc(idx_copied, 1)
                copied = b + 1
                if not isinstance(k, int):
                    copied = pool.to_reg(copied)
                pool.wait_ge(idx_loaded, 16)
                pool.wait_ge(idx_copied, copied)
                first = isinstance(k, int) and k == 0 and r == 0
                for f in range(F):
                    pool.indirect_dma_start(
                        out=gathered[:, r, f, :], out_offset=None, in_=tables[f],
                        in_offset=bass.IndirectOffsetOnAxis(ap=idx[:, r, f:f + 1].bitcast(u32), axis=0),
                    ).then_inc(first_rows_loaded[f // FPB] if first else rows_loaded[r], 16)

            def products(k, s):
                t = 2 * k + s
                pool.wait_ge(xt_ready, NG * (t + 1))
                for i, r in enumerate(POOL_ROUNDS):
                    wait(pool, round_done, NR * (t - 1) + r + 1)
                    for c in range(NC):
                        for a, b, o, n in halves(ROUNDS[r][1]):
                            last = nc.gpsimd.tensor_tensor(pool_prods[:, c, COLS * i + o:COLS * i + o + n],
                                                           xt[:, s, c, a:a + n], xt[:, s, c, b:b + n], ALU.mult)
                    last.then_inc(pool_prods_ready, 1)
                pool.wait_ge(round_done, NR * t + DVE_ROUNDS[SHARED - DVE_RING] + 1)
                for a, b, o, n in halves(ROUNDS[DVE_ROUNDS[SHARED]][1]):
                    last = nc.gpsimd.tensor_tensor(dve_prods[:, SHARED % DVE_RING, 1, o:o + n],
                                                   xt[:, s, 1, a:a + n], xt[:, s, 1, b:b + n], ALU.mult)
                last.then_inc(pool_prods_ready, 1)

            def step(k, s):
                if has(k, s, 0):
                    products(k, s)
                if has(k, s, -2):
                    gather(k + 1, s)

            gather(0, 0)
            gather(0, 1)
            periods(pool, step)

        @block.sync
        def _(sp):
            sp.dma_start(idx_all[:], ids).then_inc(idx_loaded, 16)
            for dst, src in ((ident[:], identity), (w0_sb[:], w0), (wu_sb[:], wu), (bias0_sb[:], bias0),
                             (bias12_sb[:], bias12), (pick_sb[:], pick)):
                sp.dma_start(dst, src).then_inc(consts_loaded, 16)
            sp.wait_ge(h_zeroed, 1)
            sp.dma_start(h_all[:, :, L * O:L * O + DENSE], dense).then_inc(consts_loaded, 16)
            sp.wait_ge(top_zeroed, 1)
            for dst, src in ((wt1[0:L * O + DENSE, :], w_top1), (wt2, w_top2), (wt3, w_top3),
                             (bt1, b_top1), (bt2, b_top2)):
                sp.dma_start(dst, src).then_inc(top_loaded, 16)
            sp.wait_ge(top_ready, NJOBS * len(CHUNKS))
            sp.dma_start(out, y).then_inc(stored, 16)
            sp.wait_ge(stored, 16)

        @block.vector
        def _(dve):
            nc.vector.memset(h_all[:], 0.0).then_inc(h_zeroed, 1)
            dve.wait_ge(consts_loaded, 16 * NCONST)
            nc.vector.tensor_tensor(bias0x2[:], bias0_sb[:], bias0_sb[:], ALU.add).then_inc(bias_ready, 1)

            def products(k, s, i):
                t, n_dve = 2 * k + s, len(DVE_ROUNDS)
                if i == 0:
                    dve.wait_ge(xt_ready, NG * (t + 1))
                if i >= DVE_RING:
                    dve.wait_ge(round_done, NR * t + DVE_ROUNDS[i - DVE_RING] + 1)
                else:
                    wait(dve, round_done, NR * (t - 1) + DVE_ROUNDS[i - DVE_RING] + 1)
                for c in range(1 if i == SHARED else NC):
                    for a, b, o, n in halves(ROUNDS[DVE_ROUNDS[i]][1]):
                        last = nc.vector.tensor_tensor(dve_prods[:, i % DVE_RING, c, o:o + n],
                                                       xt[:, s, c, a:a + n], xt[:, s, c, b:b + n], ALU.mult)
                last.then_inc(dve_prods_ready, 1)

            def outer_product(k, s, l):
                t = 2 * k + s
                r = (s - 1 - l) % 2
                z = (z0, z1)[l]
                dve.wait_ge((z0_ready, layer_done[0])[l], t - l)
                dve.wait_ge(ut_ready, t - l)
                wait(dve, layer_done[l], t - 1 - l)
                u = ut_sb[:, r, :].rearrange("p (f m) -> p m f", m=TILE)[:, O * l:O * (l + 1), :]
                nc.vector.tensor_tensor(
                    outer[:, l, :].rearrange("p (o f g) -> p o f g", o=O, f=F),
                    u.unsqueeze(3).to_broadcast([P, O, F, F]),
                    z[:, r, :].unsqueeze(1).unsqueeze(1).to_broadcast([P, O, F, F]),
                    ALU.mult).then_inc(outer_ready[l], 1)

            def keep(k, s, l):
                t = 2 * k + s
                lag = (1, 2, 2)[l]
                if l == 2:
                    dve.wait_ge(layer_done[1], t - 1)
                done = nc.vector.tensor_copy(h_all[:, ds(t - lag, 1), O * l:O * (l + 1)],
                                             (z0, z1, z2)[l][:, (s - lag) % 2, :].unsqueeze(1))
                if l == 2:
                    done.then_inc(kept, 1)

            def step(k, s):
                t = 2 * k + s
                if isinstance(k, int) and t == NB - 2:
                    dve.wait_ge(tr_done, NG * (NB - 1))
                    nc.vector.memset(wt1, 0.0).then_inc(top_zeroed, 1)
                if has(k, s, 0):
                    products(k, s, 0)
                    products(k, s, 1)
                if has(k, s, 1):
                    dve.wait_ge(sum_done, NR * t)
                    nc.vector.tensor_copy(zsum[:], ps_sum[(s - 1) % 2][:, 0:P]).then_inc(zsum_ready, 1)
                if has(k, s, 2):
                    outer_product(k, s, 1)
                    keep(k, s, 1)
                if has(k, s, 0):
                    products(k, s, 2)
                if has(k, s, 1):
                    dve.wait_ge(zt_done, t)
                    nc.vector.tensor_copy(z0[:, (s - 1) % 2, :],
                                          ps_sum[(s - 1) % 2][:, P:P + O]).then_inc(z0_ready, 1)
                    outer_product(k, s, 0)
                    keep(k, s, 0)
                for i in range(3, len(DVE_ROUNDS)):
                    if has(k, s, 0):
                        products(k, s, i)
                if has(k, s, 2):
                    keep(k, s, 2)

            periods(dve, step)

        @block.scalar
        def _(act):
            act.wait_ge(bias_ready, 1)

            def evacuate(k, r, g):
                b = 2 * k + r
                if g == 0:
                    wait(act, round_done, NR * (b - 1))
                act.wait_ge(tr_done, NG * b + g + 1)
                nc.scalar.activation(xt[:, r, g % NC, BANK * (g // NC):BANK * (g // NC + 1)], ps_tr[g % 2][:, :],
                                     ACT.Copy).then_inc(xt_ready, 1)

            def square(k, r, q):
                b = 2 * k + r
                if q == 0:
                    act.wait_ge(xt_ready, NG * (b + 1))
                    wait(act, round_done, NR * (b - 1) + ROUNDS.index(("act", 0)) + 1)
                c, half = divmod(q * NC, NQ)
                n = COLS * NC // NQ
                cols = slice(half * n // NC, half * n // NC + n)
                nc.scalar.activation(squares[:, c, cols], xt[:, r, c, cols], ACT.Square).then_inc(squares_ready, 1)

            def relu(k, s, r):
                t = 2 * k + s
                act.wait_ge(round_done, NR * t + r + 1)
                wait(act, sum_done, NR * t + r - BANKS + 1)
                n = BANK // 2 if ROUNDS[r][1] == F // 2 else BANK
                twice = ROUNDS[r][1] > 0
                nc.scalar.activation(relus[:, r % BANKS, 0:n], ps_round[r % BANKS][:, 0:n], ACT.Relu,
                                     bias=(bias0x2 if twice else bias0_sb)[:, 0:1],
                                     scale=2.0 if twice else 1.0).then_inc(relu_ready, 1)

            def layer(b, parity, l, o):
                if o == 0:
                    act.wait_ge(outer_ready[l], b + 1)
                pre = outer[:, l, FF * o:FF * (o + 1)]
                done = nc.scalar.activation(pre, pre, ACT.Relu, bias=bias12_sb[:, O * l + o:O * l + o + 1],
                                            accum_out=(z1, z2)[l][:, parity, o:o + 1])
                if o == O - 1:
                    done.then_inc(layer_done[l], 1)

            def top(n, j):
                if n == 0 and j == 0:
                    act.wait_ge(top_loaded, 16 * NTOP)
                first, cols = P * sum(CHUNKS[:n]), P * CHUNKS[n]
                act.wait_ge(top_done, NJOBS * n + j + 1)
                bank = ps_tr[j % 2][:, 0:cols]
                if j == 0:
                    done = nc.scalar.activation(h_in[:, 0:cols], bank, ACT.Copy)
                elif j < 5:
                    done = nc.scalar.activation(h1[:, j - 1, 0:cols], bank, ACT.Relu, bias=bt1[:, j - 1:j])
                elif j < 7:
                    done = nc.scalar.activation(h2[:, j - 5, 0:cols], bank, ACT.Relu, bias=bt2[:, j - 5:j - 4])
                else:
                    done = nc.scalar.activation(y[:, first:first + cols], bank[0:1, :], ACT.Copy)
                done.then_inc(top_ready, 1)

            def step(k, s):
                t = 2 * k + s
                for r in range(NR):
                    if has(k, s, 0):
                        relu(k, s, r)
                    if r == 1 and has(k, s, 0):
                        act.wait_ge(u_done, t + 1)
                        nc.scalar.activation(u_sb[:], ps_u[:, :], ACT.Copy).then_inc(u_copied, 1)
                    if r == 3 and has(k, s, 0):
                        act.wait_ge(ut_done, t + 1)
                        wait(act, outer_ready[1], t - 1)
                        nc.scalar.activation(ut_sb[:, s, :], ps_u[:, :], ACT.Copy).then_inc(ut_ready, 1)
                    if has(k, s, -1):
                        for g in slot(EVACUATIONS, r):
                            evacuate(k + (s + 1) // 2, (s + 1) % 2, g)
                    if has(k, s, -1):
                        for q in slot(SQUARES, r):
                            square(k + (s + 1) // 2, (s + 1) % 2, q)
                    if has(k, s, 2):
                        for o in slot(LAYER2, r):
                            layer(t - 2, s, 1, o)
                    if r == 0 and has(k, s, 2):
                        for o in layer1_slot(r):
                            layer(t - 2, s, 0, o)
                    if r > 0 and has(k, s, 1):
                        for o in layer1_slot(r):
                            layer(t - 1, (s - 1) % 2, 0, o)
                    if isinstance(k, int):
                        for n, j in TOP_SLOTS.get((t, r), ()):
                            top(n, j)

            for g in range(NG):
                evacuate(0, 0, g)
            for q in range(NQ):
                square(0, 0, q)
            periods(act, step)

        @block.tensor
        def _(pe):
            pe.wait_ge(bias_ready, 1)

            def transposes(k, r, g):
                b = 2 * k + r
                if isinstance(k, int) and b == 0:
                    pe.wait_ge(first_rows_loaded[g // NC], 16 * FPB)
                elif g == 0:
                    pe.wait_ge(rows_loaded[r], 16 * F * k + 16 * F * r)
                wait(pe, xt_ready, NG * b + g - 1)
                for i in range(FPB):
                    last = nc.tensor.transpose(ps_tr[g % 2][:, P * i:P * (i + 1)],
                                               gathered[:, r, FPB * (g // NC) + i, P * (g % NC):P * (g % NC + 1)],
                                               ident[:])
                last.then_inc(tr_done, 1)

            def contract(k, s, r):
                t = 2 * k + s
                who, d = ROUNDS[r]
                n = BANK // 2 if d == F // 2 else BANK
                if who == "act":
                    pe.wait_ge(squares_ready, NQ * (t + 1))
                    src = squares[:]
                elif who == "dve":
                    i = DVE_ROUNDS.index(r)
                    pe.wait_ge(dve_prods_ready, len(DVE_ROUNDS) * t + i + 1)
                    src = dve_prods[:, i % DVE_RING, :, :]
                else:
                    i = POOL_ROUNDS.index(r)
                    pe.wait_ge(pool_prods_ready, (len(POOL_ROUNDS) + 1) * t + i + 1)
                    src = pool_prods[:, :, COLS * i:COLS * i + NJ * n]
                wait(pe, relu_ready, NR * t + r - BANKS + 1)
                for c in range(NC):
                    if r == DVE_ROUNDS[SHARED] and c == 1:
                        pe.wait_ge(pool_prods_ready, (len(POOL_ROUNDS) + 1) * (t + 1))
                    for j in range(NJ):
                        last = nc.tensor.matmul(ps_round[r % BANKS][TILE * j:TILE * (j + 1), 0:n],
                                                w0_sb[:, c, :], src[:, c, n * j:n * (j + 1)],
                                                start=(c == 0), stop=(c == NC - 1))
                last.then_inc(round_done, 1)

            def add_up(k, s, r):
                b = 2 * k + s
                pe.wait_ge(relu_ready, NR * b + r + 1)
                if r == 0:
                    wait(pe, zsum_ready, b - 1)
                for j in range(FPB // 2 if ROUNDS[r][1] == F // 2 else FPB):
                    last = nc.tensor.matmul(ps_sum[s][TILE * j:TILE * (j + 1), 0:P], pick_sb[:],
                                            relus[:, r % BANKS, P * j:P * (j + 1)],
                                            start=(r == 0), stop=(r == NR - 1))
                last.then_inc(sum_done, 1)

            def top(n, j):
                cols = P * CHUNKS[n]
                bank = ps_tr[j % 2]
                if NJOBS * n + j >= 2:
                    pe.wait_ge(top_ready, NJOBS * n + j - 1)
                else:
                    pe.wait_ge(xt_ready, NG * NB)
                if j == 0:
                    pe.wait_ge(kept, sum(CHUNKS[:n + 1]))
                    for i in range(CHUNKS[n]):
                        last = nc.tensor.transpose(bank[:, P * i:P * (i + 1)], h_all[:, sum(CHUNKS[:n]) + i, :],
                                                   ident[:])
                elif j < 5:
                    pe.wait_ge(top_ready, NJOBS * n + 1)
                    if n == 0:
                        pe.wait_ge(top_loaded, 16 * NTOP)
                    last = nc.tensor.matmul(bank[:, 0:cols], wt1[:, P * (j - 1):P * j], h_in[:, 0:cols],
                                            start=True, stop=True)
                elif j < 7:
                    m = j - 5
                    for c in range(4):
                        pe.wait_ge(top_ready, NJOBS * n + 2 + c)
                        last = nc.tensor.matmul(bank[:, 0:cols], wt2[:, H2 * c + P * m:H2 * c + P * (m + 1)],
                                                h1[:, c, 0:cols], start=(c == 0), stop=(c == 3))
                else:
                    for m in range(2):
                        pe.wait_ge(top_ready, NJOBS * n + 6 + m)
                        last = nc.tensor.matmul(bank[0:1, 0:cols], wt3[:, m:m + 1], h2[:, m, 0:cols],
                                                start=(m == 0), stop=(m == 1))
                last.then_inc(top_done, 1)

            def step(k, s):
                t = 2 * k + s
                for r in range(NR):
                    if has(k, s, 0):
                        contract(k, s, r)
                    if r == 0 and has(k, s, 1):
                        add_up(k + (s - 1) // 2, (s - 1) % 2, NR - 1)
                    if r >= 1 and has(k, s, 0):
                        add_up(k, s, r - 1)
                    if r == 2 and has(k, s, 0):
                        pe.wait_ge(u_copied, t + 1)
                        for i in range(FPB):
                            last = nc.tensor.transpose(ps_u[:, P * i:P * (i + 1)], u_sb[:, P * i:P * (i + 1)],
                                                       ident[:])
                        last.then_inc(ut_done, 1)
                    if r == 2 and has(k, s, 1):
                        pe.wait_ge(zsum_ready, t)
                        nc.tensor.matmul(ps_sum[(s - 1) % 2][:, P:P + O], zsum[:], pick_sb[:, 0:O],
                                         start=True, stop=True).then_inc(zt_done, 1)
                    if has(k, s, -1):
                        for g in slot(EVACUATIONS, r):
                            transposes(k + (s + 1) // 2, (s + 1) % 2, g)
                    if r == 0 and has(k, s, 0):
                        wait(pe, ut_ready, t)
                        pe.wait_ge(xt_ready, NG * (t + 1))
                        for c in range(NC):
                            for j in range(NJ):
                                last = nc.tensor.matmul(ps_u[TILE * j:TILE * (j + 1), :], wu_sb[:, c, :],
                                                        xt[:, s, c, BANK * j:BANK * (j + 1)],
                                                        start=(c == 0), stop=(c == NC - 1))
                        last.then_inc(u_done, 1)
                    if isinstance(k, int):
                        for n, j in TOP_SLOTS.get((t, r), ()):
                            top(n, j)

            for g in range(NG):
                transposes(0, 0, g)
            periods(pe, step)


def kernel(**inputs):
    import numpy as np
    import concourse.bacc as bacc
    from concourse import mybir as mb
    from concourse.bass_utils import run_bass_kernel_spmd

    f4 = np.float32
    get = lambda n: np.asarray(inputs[n])
    Ws, bs = get("L0_rec_Ws"), get("L0_rec_bs")
    wt = Ws.reshape(L, O, NC, P).transpose(3, 2, 0, 1)
    w0 = np.zeros((P, NC, TILE), f4)
    w0[:, :, :O] = wt[:, :, 0]
    bias0 = np.zeros((NJ, TILE), f4)
    bias0[:, :O] = bs[0]
    pick = np.zeros((NJ, TILE, TILE), f4)
    pick[:, np.arange(O), np.arange(O)] = 1
    arrays = {f"tbl_{f}": get(f"tbl_{f}") for f in range(F)} | {
        "ids": np.ascontiguousarray(get("ids").reshape(NB, P, F).transpose(1, 0, 2)).reshape(P, NB * F),
        "dense": np.ascontiguousarray(get("dense_ctx").reshape(NB, P, DENSE).transpose(1, 0, 2)),
        "w0": w0,
        "wu": np.ascontiguousarray(wt[:, :, 1:].reshape(P, NC, TILE)),
        "bias0": bias0.reshape(P, 1),
        "bias12": np.ascontiguousarray(np.broadcast_to(bs[1:].reshape(1, 2 * O), (P, 2 * O))),
        "identity": np.eye(P, dtype=f4),
        "pick": pick.reshape(P, TILE),
        "w_top1": get("W_top1"),
        "w_top2": np.ascontiguousarray(get("W_top2").reshape(4, P, H2).transpose(1, 0, 2)).reshape(P, 4 * H2),
        "w_top3": np.ascontiguousarray(get("W_top3").reshape(2, P).T),
        "b_top1": np.ascontiguousarray(get("b_top1").reshape(4, P).T),
        "b_top2": np.ascontiguousarray(get("b_top2").reshape(2, P).T),
    }
    nc = bacc.Bacc("TRN2", target_bir_lowering=False, num_devices=1)
    aps = [nc.dram_tensor(f"in_{n}", a.shape, mb.dt.from_np(a.dtype), kind="ExternalInput").ap()
           for n, a in arrays.items()]
    out = nc.dram_tensor("out_y", (1, B), mb.dt.float32, kind="ExternalOutput").ap()
    tower(nc, aps[:F], *aps[F:], out)
    r = run_bass_kernel_spmd(nc, [{f"in_{n}": a for n, a in arrays.items()}], core_ids=[0])
    return np.asarray(r.results[0]["out_y"]).reshape(B, 1)
```

```python
import concourse.bass as bass
from concourse import mybir
from contextlib import ExitStack

B, F, E, L, O = 2048, 16, 256, 3, 16
DENSE, H1, H2 = 16, 512, 256
P = 128
NB = B // P
NC = E // P
COLS = F * P
BANK = 512
FPB = BANK // P
NJ = COLS // BANK
TILE = P // NJ
FF = F * F
ROUNDS = [("dve", 1), ("act", 0), ("dve", 2), ("dve", 3), ("pool", 7), ("dve", 4), ("pool", 8), ("dve", 5),
          ("dve", 6)]
NR = len(ROUNDS)
GROUPS = ((0, 1), (2, 3), (4, 5), (6,), (7, 8))
NGR = len(GROUPS)
DVE_ROUNDS = [r for r, (who, _) in enumerate(ROUNDS) if who == "dve"]
POOL_ROUNDS = [r for r, (who, _) in enumerate(ROUNDS) if who == "pool"]
DVE_RING = 3
BANKS = 3
NG = COLS * NC // BANK
HIN = L * O + DENSE
NQ = 4
FIRST_LOOP, LOOP_END, PERIODS = 2, (NB - 1) // 2, NB // 2
LAST = NB - 1
UNSHARED = 3
HELPED = 2
SHARED = ((5, 1, (1,)),)
LAST_SHARED = ((3, 1, (0, 1)), (4, 1, (0, 1)), (5, 1, (0, 1)))
PLAN = dict(vector=(0, 1, "zsum", 2, "z0", "layer 2", 3, "layer 1", 4, 5),
            evacuations=(0, 0, 2, 2, 2, 2, 0, 0, 0),
            squares=(0, 0, 0, 0, 0, 0, 1, 1, 2),
            layer2=(0, 0, 0, 5, 5, 4, 2, 0, 0),
            layer1=(0, 0, 0, 0, 0, 0, 2, 4, 4),
            late=(3, 3, 0, 0, 0, 0, 0, 0, 0),
            ut=3,
            outer=(3, 2))
FIRST_PLAN = PLAN | dict(vector=(0, 1, "zsum", 2, "z0", "layer 2", 3, "layer 1", "help", 4, 5))
LAST_PLAN = dict(vector=(0, 1, "zsum", 2, "z0", "layer 1", 3, "layer 2", 4, 5),
                 evacuations=(0,) * NR, squares=(0,) * NR,
                 layer2=(0, 0, 0, 0, 0, 0, 3, 3, 0),
                 layer1=(0, 0, 0, 4, 6, 6, 0, 0, 0),
                 late=PLAN["late"],
                 ut=6,
                 outer=(3, 2))
SCALAR_G = (7, 7)
CHUNKS = (4, 4, 4, 4)
NJOBS = 8
TOP_JOBS = {LAST - 1: (0, 1, 0, 0, 0, 0, 2, 2, 0), LAST: (0, 0, 1, 1, 2, 1, 1, 0, 0)}
EARLY_JOBS = 1
SCALAR_O = (10, 10)
POOL_O = 3
VECTOR_HELP = 10
OLD_O = 8
DRAIN = (("old", 3), ("top", 2), ("layer 1", 10), ("top", 2), ("old", 2), ("top", 2), ("layer 2", 4), ("top", 1),
         ("layer 2", 3), ("top", 2), ("layer 2", 3), ("top", 1), ("old", 3))


def tower(nc, tables, ids, dense, w0, wu, bias0, scale0, bias12, identity, pick, w_top1, w_top2, w_top3, b_top1,
          b_top2, out):
    f32, i32, u32 = mybir.dt.float32, mybir.dt.int32, mybir.dt.uint32
    ALU = mybir.AluOpType
    ACT = mybir.ActivationFunctionType
    AX = mybir.AxisListType
    ds = bass.ds

    ctx = ExitStack()
    with ctx:
        def sb(name, shape, dt=f32):
            return ctx.enter_context(nc.sbuf_tensor(name, shape, dt))

        def sem(name):
            return ctx.enter_context(nc.semaphore(name))

        gathered = sb("gathered", [P, 2, F, E])
        xt = sb("xt", [P, 2, NC, COLS])
        squares = sb("squares", [P, NC, COLS])
        dve_prods = sb("dve_prods", [P, DVE_RING, NC, COLS])
        pool_prods = sb("pool_prods", [P, NC, COLS + COLS // 2])
        relus = sb("relus", [P, BANKS, BANK])
        u_sb = sb("u_sb", [P, BANK])
        ut_sb = sb("ut_sb", [P, 2, BANK])
        outer = sb("outer", [P, 2, O * FF])
        zsum = sb("zsum", [P, P])
        z0 = sb("z0", [P, 2, O])
        z1 = sb("z1", [P, 2, O])
        z2 = sb("z2", [P, 2, O])
        h_all = sb("h_all", [P, NB, HIN])
        idx_all = sb("idx_all", [P, NB * F], i32)
        idx = sb("idx", [P, 2, F], i32)
        w0_sb = sb("w0_sb", [P, 2, NC, TILE])
        wu_sb = sb("wu_sb", [P, NC, TILE])
        bias0_sb = sb("bias0_sb", [P, 1])
        bias0x2 = sb("bias0x2", [P, 1])
        bias_first = sb("bias_first", [P, 1])
        scale_first = sb("scale_first", [P, 1])
        bias12_sb = sb("bias12_sb", [P, 2 * O])
        ident = sb("ident", [P, P])
        pick_sb = sb("pick_sb", [P, 2, TILE])
        h2 = sb("h2", [P, 2, BANK])
        y = u_sb[:, 0:P]
        wt3 = idx_all[:, 0:2 * TILE].bitcast(f32).rearrange("p (m n) -> p m n", m=2)
        bt1 = sb("bt1", [P, 4])
        bt2 = sb("bt2", [P, 2])
        zero = sb("zero", [P, 1])
        wt1 = gathered[:, 0, 0:2, :].rearrange("p a b -> p (a b)")
        wt2 = gathered[:, 0, 2:6, :].rearrange("p k n -> p (k n)")
        h_in = gathered[:, 0, 6:8, :].rearrange("p a b -> p (a b)")
        h1 = gathered[:, 0, 8:16, :].rearrange("p (m a) b -> p m (a b)", m=4)
        old_outer = squares[:].rearrange("p c n -> p (c n)")

        ps = [ctx.enter_context(nc.psum_tensor(f"ps{i}", [P, BANK], f32)) for i in range(8)]
        ps_round, ps_tr, ps_sum, ps_u = ps[0:BANKS], ps[3:5], ps[5:7], ps[7]

        idx_loaded = sem("idx_loaded")
        idx_copied = sem("idx_copied")
        rows_loaded = [sem("rows_loaded0"), sem("rows_loaded1")]
        first_rows_loaded = [sem(f"first_rows_loaded{i}") for i in range(NJ)]
        consts_loaded = sem("consts_loaded")
        bias_ready = sem("bias_ready")
        tr_done = sem("tr_done")
        xt_ready = sem("xt_ready")
        squares_ready = sem("squares_ready")
        dve_prods_ready = sem("dve_prods_ready")
        pool_prods_ready = sem("pool_prods_ready")
        help_ready = sem("help_ready")
        shared_ready = sem("shared_ready")
        round_done = sem("round_done")
        relu_ready = sem("relu_ready")
        sum_done = sem("sum_done")
        zsum_ready = sem("zsum_ready")
        zt_done = sem("zt_done")
        z0_ready = sem("z0_ready")
        u_done = sem("u_done")
        u_copied = sem("u_copied")
        ut_done = sem("ut_done")
        ut_ready = sem("ut_ready")
        outer_ready = [sem("outer1_ready"), sem("outer2_ready")]
        layer_done = [sem("layer1_done"), sem("layer2_done")]
        scalar_outer_ready = [sem("scalar_outer1_ready"), sem("scalar_outer2_ready")]
        old_outer_ready = sem("old_outer_ready")
        old_layer_done = sem("old_layer_done")
        pool_outer_ready = sem("pool_outer_ready")
        vector_layer_done = sem("vector_layer_done")
        kept = sem("kept")
        top_zeroed = sem("top_zeroed")
        top_loaded = sem("top_loaded")
        top_done = sem("top_done")
        top_ready = sem("top_ready")
        stored = sem("stored")

        block = ctx.enter_context(nc.Block())
        NCONST, NTOP = 8, 5

        def periods(eng, step):
            for k in range(FIRST_LOOP):
                for s in range(2):
                    step(k, s)
            with eng.Fori(FIRST_LOOP, LOOP_END) as k:
                for s in range(2):
                    step(k, s)
            for k in range(LOOP_END, PERIODS):
                for s in range(2):
                    step(k, s)

        def helped(t):
            return isinstance(t, int) and t < HELPED

        def plan(k, s):
            return FIRST_PLAN if helped(2 * k + s) else LAST_PLAN if isinstance(k, int) and 2 * k + s == LAST else PLAN

        def top_jobs(k, s, r):
            if not isinstance(k, int) or 2 * k + s not in TOP_JOBS:
                return []
            t = 2 * k + s
            start = sum(TOP_JOBS[LAST - 1]) * (t == LAST) + sum(TOP_JOBS[t][:r])
            return [divmod(i, NJOBS) for i in range(start, start + TOP_JOBS[t][r])]

        first_drain_job = sum(map(sum, TOP_JOBS.values()))
        drain_banks = [ps_tr[0], ps_tr[1], ps_u, ps_round[2]]

        def bank_of(job):
            if job < first_drain_job:
                return ps_tr[job % 2], job - 2
            before = job - 4
            if before < first_drain_job and job % 4 < 2:
                before = first_drain_job - 1 - (first_drain_job - 1 - job) % 2
            return drain_banks[job % 4], before if before >= first_drain_job or job % 4 < 2 else None

        def shared(t):
            if not isinstance(t, int):
                return SHARED
            return () if t < UNSHARED else SHARED if t < LAST - 1 else LAST_SHARED

        def shared_count(t, i):
            before = t - UNSHARED if not isinstance(t, int) or t < LAST else LAST - 1 - UNSHARED + len(LAST_SHARED)
            return before + [part[0] for part in shared(t)].index(i) + 1

        ENDS = [group[-1] for group in GROUPS]

        def columns(g):
            return BANK // 2 if ROUNDS[GROUPS[g][0]][1] == F // 2 else BANK

        def former(t, g):
            if g >= BANKS:
                return NGR * t + g - BANKS + 1
            return NGR * (t - 1) + max(h for h in range(NGR) if h % BANKS == g) + 1

        def outer_view(l, o, n):
            return outer[:, l, FF * o:FF * (o + n)].rearrange("p (o f g) -> p o f g", o=n, f=F)

        def u_view(r, l, o, n):
            u = ut_sb[:, r, :].rearrange("p (f m) -> p m f", m=TILE)[:, O * l + o:O * l + o + n, :]
            return u.unsqueeze(3).to_broadcast([P, n, F, F])

        def z_view(z, r, n):
            return z[:, r, :].unsqueeze(1).unsqueeze(1).to_broadcast([P, n, F, F])

        def vector_g(b, l):
            return F - SCALAR_G[l] if not isinstance(b, int) or b < LAST - 2 - l else F

        def has(k, s, lag):
            return not isinstance(k, int) or 0 <= 2 * k + s - lag < NB

        def wait(eng, semaphore, value):
            if not isinstance(value, int) or value > 0:
                eng.wait_ge(semaphore, value)

        def slot(table, r):
            return range(sum(table[:r]), sum(table[:r + 1]))


        def halves(d):
            if d == F // 2:
                return [(0, d * P, 0, d * P)]
            return [(0, d * P, 0, (F - d) * P), ((F - d) * P, 0, (F - d) * P, d * P)]

        @block.gpsimd
        def _(pool):
            pool.wait_ge(idx_loaded, 16)

            def gather(k, r):
                b = 2 * k + r
                if not (isinstance(k, int) and k == 0):
                    used = NG * (b - 1)
                    pool.wait_ge(tr_done, used)
                nc.gpsimd.tensor_copy(idx[:, r, :], idx_all[:, ds(F * b, F)]).then_inc(idx_copied, 1)
                copied = b + 1
                if not isinstance(k, int):
                    copied = pool.to_reg(copied)
                pool.wait_ge(idx_loaded, 16)
                pool.wait_ge(idx_copied, copied)
                first = isinstance(k, int) and k == 0 and r == 0
                for f in range(F):
                    pool.indirect_dma_start(
                        out=gathered[:, r, f, :], out_offset=None, in_=tables[f],
                        in_offset=bass.IndirectOffsetOnAxis(ap=idx[:, r, f:f + 1].bitcast(u32), axis=0),
                    ).then_inc(first_rows_loaded[f // FPB] if first else rows_loaded[r], 16)

            def products(k, s):
                t = 2 * k + s
                pool.wait_ge(xt_ready, NG * (t + 1))
                for i, r in enumerate(POOL_ROUNDS[:1] if helped(t) else POOL_ROUNDS):
                    wait(pool, round_done, NR * (t - 1) + r + 1)
                    for c in range(NC):
                        for a, b, o, n in halves(ROUNDS[r][1]):
                            last = nc.gpsimd.tensor_tensor(pool_prods[:, c, COLS * i + o:COLS * i + o + n],
                                                           xt[:, s, c, a:a + n], xt[:, s, c, b:b + n], ALU.mult)
                    last.then_inc(pool_prods_ready, 1)
                for i, c, ranges in shared(t):
                    pool.wait_ge(round_done, NR * t + DVE_ROUNDS[i - DVE_RING] + 1)
                    for a, b, o, n in [halves(ROUNDS[DVE_ROUNDS[i]][1])[x] for x in ranges]:
                        last = nc.gpsimd.tensor_tensor(dve_prods[:, i % DVE_RING, c, o:o + n],
                                                       xt[:, s, c, a:a + n], xt[:, s, c, b:b + n], ALU.mult)
                    last.then_inc(shared_ready, 1)

            def step(k, s):
                if has(k, s, 0):
                    products(k, s)
                if has(k, s, -2):
                    gather(k + 1, s)

            gather(0, 0)
            gather(0, 1)
            periods(pool, step)
            r = (LAST - 1) % 2
            pool.wait_ge(round_done, NR * LAST + ROUNDS.index(("act", 0)) + 1)
            pool.wait_ge(ut_ready, LAST)
            pool.wait_ge(layer_done[0], LAST)
            nc.gpsimd.tensor_tensor(old_outer.rearrange("p (o f g) -> p o f g", o=O, f=F), u_view(r, 1, 0, O),
                                    z_view(z1, r, O), ALU.mult).then_inc(old_outer_ready, 1)
            r = LAST % 2
            pool.wait_ge(ut_ready, NB)
            for l in range(2):
                pool.wait_ge(layer_done[l], NB - 1 - l)
                pool.wait_ge((z0_ready, layer_done[0])[l], NB)
                if l:
                    pool.wait_ge(vector_layer_done, 2)
                nc.gpsimd.tensor_tensor(outer_view(l, O - POOL_O, POOL_O), u_view(r, l, O - POOL_O, POOL_O),
                                        z_view((z0, z1)[l], r, POOL_O), ALU.mult).then_inc(pool_outer_ready, 1)

        @block.sync
        def _(sp):
            sp.dma_start(idx_all[:], ids).then_inc(idx_loaded, 16)
            for dst, src in ((ident[:], identity), (w0_sb[:], w0), (wu_sb[:], wu), (bias0_sb[:], bias0),
                             (scale_first[:], scale0), (bias12_sb[:], bias12), (pick_sb[:], pick)):
                sp.dma_start(dst, src).then_inc(consts_loaded, 16)
            sp.dma_start(h_all[:, :, L * O:L * O + DENSE], dense).then_inc(consts_loaded, 16)
            sp.wait_ge(top_zeroed, 1)
            sp.wait_ge(idx_copied, NB)
            for dst, src in ((wt1[0:HIN, :], w_top1), (wt2, w_top2), (wt3, w_top3),
                             (bt1[:], b_top1), (bt2[:], b_top2)):
                sp.dma_start(dst, src).then_inc(top_loaded, 16)
            for n, size in enumerate(CHUNKS):
                sp.wait_ge(top_ready, NJOBS * (n + 1))
                sp.dma_start(out[sum(CHUNKS[:n]):sum(CHUNKS[:n + 1]), :],
                             y[0:TILE * size:TILE, :]).then_inc(stored, 16)
            sp.wait_ge(stored, 16 * len(CHUNKS))

        @block.vector
        def _(dve):
            
            nc.vector.memset(zero[:], 0.0)
            dve.wait_ge(consts_loaded, 16 * NCONST)
            nc.vector.tensor_tensor(bias0x2[:], bias0_sb[:], bias0_sb[:], ALU.add)
            nc.vector.tensor_tensor(bias_first[:], bias0_sb[:], scale_first[:], ALU.mult).then_inc(bias_ready, 1)

            def products(k, s, i):
                t, n_dve = 2 * k + s, len(DVE_ROUNDS)
                if i == 0:
                    dve.wait_ge(xt_ready, NG * (t + 1))
                if i >= DVE_RING:
                    dve.wait_ge(round_done, NR * t + DVE_ROUNDS[i - DVE_RING] + 1)
                else:
                    wait(dve, round_done, NR * (t - 1) + DVE_ROUNDS[i - DVE_RING] + 1)
                for c in range(NC):
                    given = [x for part in shared(t) if part[:2] == (i, c) for x in part[2]]
                    for a, b, o, n in [h for x, h in enumerate(halves(ROUNDS[DVE_ROUNDS[i]][1])) if x not in given]:
                        last = nc.vector.tensor_tensor(dve_prods[:, i % DVE_RING, c, o:o + n],
                                                       xt[:, s, c, a:a + n], xt[:, s, c, b:b + n], ALU.mult)
                last.then_inc(dve_prods_ready, 1)

            def first_products():
                for m in range(NJ):
                    dve.wait_ge(xt_ready, NC * (m + 1))
                    for i in range(DVE_RING):
                        d = ROUNDS[DVE_ROUNDS[i]][1]
                        parts = [(max(0, FPB * m - d), max(0, FPB * m - d) + d, FPB * (m + 1) - d)]
                        if m == NJ - 1:
                            parts.append((F - d, 0, F))
                        for c in range(NC):
                            for f, g, end in parts:
                                n = P * (end - f)
                                last = nc.vector.tensor_tensor(
                                    dve_prods[:, i, c, P * f:P * end], xt[:, 0, c, P * f:P * end],
                                    xt[:, 0, c, P * g:P * g + n], ALU.mult)
                        if m == NJ - 1:
                            last.then_inc(dve_prods_ready, 1)

            def outer_product(k, s, l):
                t = 2 * k + s
                r = (s - 1 - l) % 2
                z = (z0, z1)[l]
                dve.wait_ge((z0_ready, layer_done[0])[l], t - l)
                dve.wait_ge(ut_ready, t - l)
                wait(dve, layer_done[l], t - 1 - l)
                g = vector_g(t - 1 - l, l)
                nc.vector.tensor_tensor(outer_view(l, 0, O)[:, :, :, 0:g], u_view(r, l, 0, O)[:, :, :, 0:g],
                                        z_view(z, r, O)[:, :, :, 0:g], ALU.mult).then_inc(outer_ready[l], 1)

            def keep(k, s, l):
                t = 2 * k + s
                lag = l + 1
                if l == 2:
                    dve.wait_ge(layer_done[1], t - 2)
                done = nc.vector.tensor_copy(h_all[:, ds(t - lag, 1), O * l:O * (l + 1)],
                                             (z0, z1, z2)[l][:, (s - lag) % 2, :].unsqueeze(1))
                if l == 2:
                    done.then_inc(kept, 1)

            def step(k, s):
                t = 2 * k + s
                if isinstance(k, int) and t == LAST - 1:
                    dve.wait_ge(tr_done, NG * LAST)
                    nc.vector.memset(h_in, 0.0)
                    nc.vector.memset(wt1, 0.0).then_inc(top_zeroed, 1)
                for part in plan(k, s)["vector"]:
                    if part == "zsum":
                        if has(k, s, 1):
                            dve.wait_ge(sum_done, NGR * t)
                            nc.vector.tensor_copy(zsum[:], ps_sum[(s - 1) % 2][:, 0:P]).then_inc(zsum_ready, 1)
                    elif part == "help":
                        wait(dve, round_done, NR * (t - 1) + POOL_ROUNDS[1] + 1)
                        for c in range(NC):
                            for a, b, o, n in halves(ROUNDS[POOL_ROUNDS[1]][1]):
                                last = nc.vector.tensor_tensor(pool_prods[:, c, COLS + o:COLS + o + n],
                                                               xt[:, s, c, a:a + n], xt[:, s, c, b:b + n], ALU.mult)
                        last.then_inc(help_ready, 1)
                    elif part == "layer 2":
                        if has(k, s, 2):
                            outer_product(k, s, 1)
                            keep(k, s, 1)
                        if has(k, s, 3):
                            keep(k, s, 2)
                    elif part == "z0":
                        if has(k, s, 1):
                            dve.wait_ge(zt_done, t)
                            nc.vector.tensor_copy(z0[:, (s - 1) % 2, :],
                                                  ps_sum[(s - 1) % 2][:, P:P + O]).then_inc(z0_ready, 1)
                    elif part == "layer 1":
                        if has(k, s, 1):
                            outer_product(k, s, 0)
                            keep(k, s, 0)
                    elif has(k, s, 0) and not (isinstance(k, int) and t == 0 and part < DVE_RING):
                        products(k, s, part)

            first_products()
            periods(dve, step)
            def layer(b, l, o):
                pre = (old_outer if b == LAST - 1 else outer[:, l, :])[:, FF * o:FF * (o + 1)]
                return nc.vector.scalar_tensor_tensor(
                    out=pre, in0=pre, scalar=bias12_sb[:, O * l + o:O * l + o + 1],
                    in1=zero[:, 0:1].to_broadcast([P, FF]), op0=ALU.add, op1=ALU.max,
                    accum_out=(z1, z2)[l][:, b % 2, o:o + 1])

            def keep_last(b, l):
                if l == 2:
                    if b == LAST - 1:
                        dve.wait_ge(old_layer_done, 1)
                    else:
                        dve.wait_ge(layer_done[1], LAST if b == LAST else b + 1)
                done = nc.vector.tensor_copy(h_all[:, b:b + 1, O * l:O * (l + 1)],
                                             (z0, z1, z2)[l][:, b % 2, :].unsqueeze(1))
                if l == 2:
                    done.then_inc(kept, 1)

            dve.wait_ge(outer_ready[1], LAST - 1)
            for o in range(O - VECTOR_HELP, O):
                done = layer(LAST - 2, 1, o)
            done.then_inc(vector_layer_done, 1)
            dve.wait_ge(sum_done, NGR * NB)
            nc.vector.tensor_copy(zsum[:], ps_sum[LAST % 2][:, 0:P]).then_inc(zsum_ready, 1)
            dve.wait_ge(zt_done, NB)
            nc.vector.tensor_copy(z0[:, LAST % 2, :], ps_sum[LAST % 2][:, P:P + O]).then_inc(z0_ready, 1)
            dve.wait_ge(vector_layer_done, 1)
            keep_last(LAST - 2, 2)
            dve.wait_ge(ut_ready, NB)
            for l in range(2):
                dve.wait_ge((z0_ready, layer_done[0])[l], NB)
                if l:
                    dve.wait_ge(vector_layer_done, 2)
                dve.wait_ge(layer_done[l], NB - 1 - l)
                for o, n in ((0, SCALAR_O[l]), (SCALAR_O[l], O - POOL_O - SCALAR_O[l])):
                    nc.vector.tensor_tensor(outer_view(l, o, n), u_view(LAST % 2, l, o, n),
                                            z_view((z0, z1)[l], LAST % 2, n), ALU.mult).then_inc(outer_ready[l], 1)
                dve.wait_ge(outer_ready[l], NB + 1 - l)
                for o in range(SCALAR_O[l], O):
                    if o == O - POOL_O:
                        dve.wait_ge(pool_outer_ready, l + 1)
                    done = layer(LAST, l, o)
                done.then_inc(vector_layer_done, 1)
            dve.wait_ge(old_outer_ready, 1)
            for o in range(OLD_O, O):
                done = layer(LAST - 1, 1, o)
            done.then_inc(vector_layer_done, 1)
            dve.wait_ge(vector_layer_done, 4)
            for b, l in ((LAST, 0), (LAST - 1, 1), (LAST, 1), (LAST - 1, 2)):
                keep_last(b, l)
            keep_last(LAST, 2)

        @block.scalar
        def _(act):
            act.wait_ge(bias_ready, 1)

            def evacuate(k, r, g):
                b = 2 * k + r
                if g == 0:
                    wait(act, round_done, NR * (b - 1))
                act.wait_ge(tr_done, NG * b + g + 1)
                nc.scalar.activation(xt[:, r, g % NC, BANK * (g // NC):BANK * (g // NC + 1)], ps_tr[g % 2][:, :],
                                     ACT.Copy).then_inc(xt_ready, 1)

            def square(k, r, q):
                b = 2 * k + r
                if q == 0:
                    act.wait_ge(xt_ready, NG * (b + 1))
                    wait(act, round_done, NR * (b - 1) + ROUNDS.index(("act", 0)) + 1)
                c, half = divmod(q * NC, NQ)
                n = COLS * NC // NQ
                cols = slice(half * n // NC, half * n // NC + n)
                nc.scalar.activation(squares[:, c, cols], xt[:, r, c, cols], ACT.Square).then_inc(squares_ready, 1)

            def relu(k, s, g):
                t = 2 * k + s
                act.wait_ge(round_done, NR * t + GROUPS[g][-1] + 1)
                wait(act, sum_done, former(t, g))
                n = columns(g)
                nc.scalar.activation(relus[:, g % BANKS, 0:n], ps_round[g % BANKS][:, 0:n], ACT.Relu,
                                     bias=(bias0x2 if g else bias_first)[:, 0:1],
                                     scale=2.0 if g else scale_first[:, 0:1]).then_inc(relu_ready, 1)

            def scalar_products(b, parity, l):
                first = vector_g(b, l)
                if first == F:
                    return
                act.wait_ge((z0_ready, layer_done[0])[l], b + 1)
                wait(act, layer_done[l], b)
                for g in range(first, F):
                    done = nc.scalar.activation(
                        outer_view(l, 0, O)[:, :, :, g],
                        ut_sb[:, parity, :].rearrange("p (f m) -> p m f", m=TILE)[:, O * l:O * (l + 1), :],
                        ACT.Copy, scale=(z0, z1)[l][:, parity, g:g + 1])
                done.then_inc(scalar_outer_ready[l], 1)

            def layer(b, parity, l, o, products=None, last_o=O - 1):
                if o == 0 and products is None and vector_g(b, l) < F:
                    act.wait_ge(scalar_outer_ready[l], b + 1)
                if o == 0:
                    if products is None:
                        act.wait_ge(outer_ready[l], b + 1 if l == 0 or not isinstance(b, int) or b < LAST else b)
                    else:
                        act.wait_ge(old_outer_ready, 1)
                pre = (outer[:, l, :] if products is None else products)[:, FF * o:FF * (o + 1)]
                done = nc.scalar.activation(pre, pre, ACT.Relu, bias=bias12_sb[:, O * l + o:O * l + o + 1],
                                            accum_out=(z1, z2)[l][:, parity, o:o + 1])
                if o == (O - 1 - VECTOR_HELP if l == 1 and isinstance(b, int) and b == LAST - 2 else last_o):
                    done.then_inc(layer_done[l] if products is None else old_layer_done, 1)

            def top(n, j):
                if n == 0 and j == 1:
                    act.wait_ge(top_loaded, 16 * NTOP)
                cols = P * CHUNKS[n]
                act.wait_ge(top_done, NJOBS * n + j + 1)
                bank = bank_of(NJOBS * n + j)[0][:, 0:cols]
                if j == 0:
                    done = nc.scalar.activation(h_in[0:HIN, 0:cols], bank[0:HIN, :], ACT.Copy)
                elif j < 5:
                    done = nc.scalar.activation(h1[:, j - 1, 0:cols], bank, ACT.Relu, bias=bt1[:, j - 1:j])
                elif j < 7:
                    done = nc.scalar.activation(h2[:, j - 5, 0:cols], bank, ACT.Relu, bias=bt2[:, j - 5:j - 4])
                else:
                    if n:
                        act.wait_ge(stored, 16 * n)
                    done = nc.scalar.activation(y[0:TILE * CHUNKS[n], :], bank[0:TILE * CHUNKS[n], 0:P], ACT.Copy)
                done.then_inc(top_ready, 1)

            def step(k, s):
                t = 2 * k + s
                for r in range(NR):
                    if has(k, s, 0) and r in ENDS:
                        relu(k, s, ENDS.index(r))
                    for n, j in top_jobs(k, s, r - 1) if r else ():
                        top(n, j)
                    if r == 1 and has(k, s, 0):
                        act.wait_ge(u_done, t + 1)
                        nc.scalar.activation(u_sb[:], ps_u[:, :], ACT.Copy).then_inc(u_copied, 1)
                    if r == plan(k, s)["ut"] and has(k, s, 0):
                        act.wait_ge(ut_done, t + 1)
                        if vector_g(t - 2, 1) < F:
                            wait(act, scalar_outer_ready[1], t - 1)
                        wait(act, outer_ready[1], t - 1)
                        nc.scalar.activation(ut_sb[:, s, :], ps_u[:, :], ACT.Copy).then_inc(ut_ready, 1)
                    if has(k, s, -1):
                        for g in slot(plan(k, s)["evacuations"], r):
                            evacuate(k + (s + 1) // 2, (s + 1) % 2, g)
                    if has(k, s, -1):
                        for q in slot(plan(k, s)["squares"], r):
                            square(k + (s + 1) // 2, (s + 1) % 2, q)
                    if r == plan(k, s)["outer"][1] and has(k, s, 2):
                        scalar_products(t - 2, s, 1)
                    if r == plan(k, s)["outer"][0] and has(k, s, 1):
                        scalar_products(t - 1, (s - 1) % 2, 0)
                    if has(k, s, 2):
                        for o in slot(plan(k, s)["layer2"], r):
                            layer(t - 2, s, 1, o)
                    if has(k, s, 2):
                        for o in slot(plan(k, s)["late"], r):
                            layer(t - 2, s, 0, O - sum(PLAN["late"]) + o)
                    if has(k, s, 1):
                        for o in slot(plan(k, s)["layer1"], r):
                            layer(t - 1, (s - 1) % 2, 0, o)

            for g in range(NG):
                evacuate(0, 0, g)
            for q in range(NQ):
                square(0, 0, q)
            periods(act, step)
            job, old, new = first_drain_job, 0, [0, 0]
            for what, count in DRAIN + (("top", NJOBS * len(CHUNKS)),):
                for _ in range(count):
                    if what == "top" and job < NJOBS * len(CHUNKS):
                        top(*divmod(job, NJOBS))
                        job += 1
                    elif what == "old":
                        layer(LAST - 1, (LAST - 1) % 2, 1, old, old_outer, last_o=OLD_O - 1)
                        old += 1
                    elif what != "top":
                        l = int(what[-1]) - 1
                        layer(LAST, LAST % 2, l, new[l], last_o=SCALAR_O[l] - 1)
                        new[l] += 1

        @block.tensor
        def _(pe):
            pe.wait_ge(bias_ready, 1)

            def transposes(k, r, g):
                b = 2 * k + r
                if isinstance(k, int) and b == 0:
                    pe.wait_ge(first_rows_loaded[g // NC], 16 * FPB)
                elif g == 0:
                    pe.wait_ge(rows_loaded[r], 16 * F * k + 16 * F * r)
                wait(pe, xt_ready, NG * b + g - 1)
                if isinstance(k, int) and b == LAST and g == 0:
                    pe.wait_ge(top_ready, EARLY_JOBS)
                for i in range(FPB):
                    last = nc.tensor.transpose(ps_tr[g % 2][:, P * i:P * (i + 1)],
                                               gathered[:, r, FPB * (g // NC) + i, P * (g % NC):P * (g % NC + 1)],
                                               ident[:])
                last.then_inc(tr_done, 1)

            def contract(k, s, r):
                t = 2 * k + s
                who, d = ROUNDS[r]
                n = BANK // 2 if d == F // 2 else BANK
                if who == "act":
                    pe.wait_ge(squares_ready, NQ * (t + 1))
                    src = squares[:]
                elif who == "dve":
                    i = DVE_ROUNDS.index(r)
                    pe.wait_ge(dve_prods_ready, len(DVE_ROUNDS) * t + i + 1)
                    src = dve_prods[:, i % DVE_RING, :, :]
                else:
                    i = POOL_ROUNDS.index(r)
                    if i and helped(t):
                        pe.wait_ge(help_ready, t + 1)
                    else:
                        pe.wait_ge(pool_prods_ready, t + 1 if helped(t) else len(POOL_ROUNDS) * t - HELPED + i + 1)
                    src = pool_prods[:, :, COLS * i:COLS * i + NJ * n]
                g = [r in group for group in GROUPS].index(True)
                part = GROUPS[g].index(r)
                if part == 0:
                    wait(pe, relu_ready, former(t, g))
                for c in range(NC):
                    if who == "dve" and (i, c) in [part[:2] for part in shared(t)]:
                        pe.wait_ge(shared_ready, shared_count(t, i))
                    for j in range(NJ):
                        last = nc.tensor.matmul(ps_round[g % BANKS][TILE * j:TILE * (j + 1), 0:n],
                                                w0_sb[:, part, c, :], src[:, c, n * j:n * (j + 1)],
                                                start=(part == c == 0), stop=(r in ENDS and c == NC - 1))
                last.then_inc(round_done, 1)

            def add_up(k, s, g):
                b = 2 * k + s
                pe.wait_ge(relu_ready, NGR * b + g + 1)
                if g == 0:
                    wait(pe, zsum_ready, b - 1)
                for j in range(columns(g) // P):
                    last = nc.tensor.matmul(ps_sum[s][TILE * j:TILE * (j + 1), 0:P], pick_sb[:, len(GROUPS[g]) - 1, :],
                                            relus[:, g % BANKS, P * j:P * (j + 1)],
                                            start=(g == 0), stop=(g == NGR - 1))
                last.then_inc(sum_done, 1)

            def top(n, j):
                cols = P * CHUNKS[n]
                job = NJOBS * n + j
                bank, before = bank_of(job)
                if before is None:
                    pe.wait_ge(ut_ready, NB)
                    pe.wait_ge(relu_ready, NGR * NB)
                elif before >= 0:
                    pe.wait_ge(top_ready, before + 1)
                if job in (0, EARLY_JOBS):
                    pe.wait_ge(xt_ready, NG * (LAST if job == 0 else NB))
                if j == 0:
                    pe.wait_ge(kept, sum(CHUNKS[:n + 1]))
                    for i in range(CHUNKS[n]):
                        last = nc.tensor.transpose(bank[0:HIN, P * i:P * (i + 1)], h_all[:, sum(CHUNKS[:n]) + i, :],
                                                   ident[:])
                elif j < 5:
                    pe.wait_ge(top_ready, NJOBS * n + 1)
                    if n == 0 and j == 1:
                        pe.wait_ge(top_loaded, 16 * NTOP)
                    last = nc.tensor.matmul(bank[:, 0:cols], wt1[:, P * (j - 1):P * j], h_in[:, 0:cols],
                                            start=True, stop=True)
                elif j < 7:
                    m = j - 5
                    for c in range(4):
                        pe.wait_ge(top_ready, NJOBS * n + 2 + c)
                        last = nc.tensor.matmul(bank[:, 0:cols], wt2[:, H2 * c + P * m:H2 * c + P * (m + 1)],
                                                h1[:, c, 0:cols], start=(c == 0), stop=(c == 3))
                else:
                    for m in range(2):
                        pe.wait_ge(top_ready, NJOBS * n + 6 + m)
                        for i in range(CHUNKS[n]):
                            last = nc.tensor.matmul(bank[TILE * i:TILE * (i + 1), 0:P], wt3[:, m, :],
                                                    h2[:, m, P * i:P * (i + 1)], start=(m == 0), stop=(m == 1))
                last.then_inc(top_done, 1)

            def step(k, s):
                t = 2 * k + s
                for r in range(NR):
                    if has(k, s, 0):
                        contract(k, s, r)
                    if r == 0 and has(k, s, 1):
                        add_up(k + (s - 1) // 2, (s - 1) % 2, NGR - 1)
                    if r - 1 in ENDS and has(k, s, 0):
                        add_up(k, s, ENDS.index(r - 1))
                    if r == 2 and has(k, s, 0):
                        pe.wait_ge(u_copied, t + 1)
                        for i in range(FPB):
                            last = nc.tensor.transpose(ps_u[:, P * i:P * (i + 1)], u_sb[:, P * i:P * (i + 1)],
                                                       ident[:])
                        last.then_inc(ut_done, 1)
                    if r == 1 and has(k, s, 1):
                        pe.wait_ge(zsum_ready, t)
                        nc.tensor.matmul(ps_sum[(s - 1) % 2][:, P:P + O], zsum[:], pick_sb[:, 0, 0:O],
                                         start=True, stop=True).then_inc(zt_done, 1)
                    if has(k, s, -1):
                        for g in slot(plan(k, s)["evacuations"], r):
                            transposes(k + (s + 1) // 2, (s + 1) % 2, g)
                    if r == 0 and has(k, s, 0):
                        wait(pe, ut_ready, t)
                        pe.wait_ge(xt_ready, NG * (t + 1))
                        for c in range(NC):
                            for j in range(NJ):
                                last = nc.tensor.matmul(ps_u[TILE * j:TILE * (j + 1), :], wu_sb[:, c, :],
                                                        xt[:, s, c, BANK * j:BANK * (j + 1)],
                                                        start=(c == 0), stop=(c == NC - 1))
                        last.then_inc(u_done, 1)
                    for n, j in top_jobs(k, s, r):
                        top(n, j)

            for g in range(NG):
                transposes(0, 0, g)
            periods(pe, step)
            for job in range(first_drain_job, NJOBS * len(CHUNKS)):
                if job == first_drain_job:
                    add_up(LAST // 2, LAST % 2, NGR - 1)
                    pe.wait_ge(zsum_ready, NB)
                    nc.tensor.matmul(ps_sum[LAST % 2][:, P:P + O], zsum[:], pick_sb[:, 0, 0:O],
                                     start=True, stop=True).then_inc(zt_done, 1)
                top(*divmod(job, NJOBS))


def kernel(**inputs):
    import numpy as np
    import concourse.bacc as bacc
    from concourse import mybir as mb
    from concourse.bass_utils import run_bass_kernel_spmd

    f4 = np.float32
    get = lambda n: np.asarray(inputs[n])
    Ws, bs = get("L0_rec_Ws"), get("L0_rec_bs")
    wt = Ws.reshape(L, O, NC, P).transpose(3, 2, 0, 1)
    w0 = np.zeros((P, 2, NC, TILE), f4)
    w0[:, 0, :, :O] = w0[:, 1, :, O:] = wt[:, :, 0]
    w_top3 = np.zeros((P, 2, TILE), f4)
    w_top3[:, :, 0] = get("W_top3").reshape(2, P).T
    scale0 = np.ones((NJ, TILE), f4)
    scale0[:, :O] = 2
    pick = np.zeros((NJ, TILE, 2, TILE), f4)
    o = np.arange(O)
    pick[:, o, :, o] = 1
    pick[:, O + o, 1, o] = 1
    arrays = {f"tbl_{f}": get(f"tbl_{f}") for f in range(F)} | {
        "ids": np.ascontiguousarray(get("ids").reshape(NB, P, F).transpose(1, 0, 2)).reshape(P, NB * F),
        "dense": np.ascontiguousarray(get("dense_ctx").reshape(NB, P, DENSE).transpose(1, 0, 2)),
        "w0": w0,
        "wu": np.ascontiguousarray(wt[:, :, 1:].reshape(P, NC, TILE)),
        "bias0": np.ascontiguousarray(np.broadcast_to(bs[0], (P // O, O))).reshape(P, 1),
        "scale0": scale0.reshape(P, 1),
        "bias12": np.ascontiguousarray(np.broadcast_to(bs[1:].reshape(1, 2 * O), (P, 2 * O))),
        "identity": np.eye(P, dtype=f4),
        "pick": pick.reshape(P, 2, TILE),
        "w_top1": get("W_top1"),
        "w_top2": np.ascontiguousarray(get("W_top2").reshape(4, P, H2).transpose(1, 0, 2)).reshape(P, 4 * H2),
        "w_top3": w_top3,
        "b_top1": np.ascontiguousarray(get("b_top1").reshape(4, P).T),
        "b_top2": np.ascontiguousarray(get("b_top2").reshape(2, P).T),
    }
    nc = bacc.Bacc("TRN2", target_bir_lowering=False, num_devices=1)
    aps = [nc.dram_tensor(f"in_{n}", a.shape, mb.dt.from_np(a.dtype), kind="ExternalInput").ap()
           for n, a in arrays.items()]
    out = nc.dram_tensor("out_y", (NB, P), mb.dt.float32, kind="ExternalOutput").ap()
    tower(nc, aps[:F], *aps[F:], out)
    r = run_bass_kernel_spmd(nc, [{f"in_{n}": a for n, a in arrays.items()}], core_ids=[0])
    return np.asarray(r.results[0]["out_y"]).reshape(B, 1)
```
